# Optimizing a Trainium2 kernel written in Bass

```python
import numpy as np
import jax
import jax.numpy as jnp

def _softmax(x, axis=-1):
    return jax.nn.softmax(x, axis=axis)

def _gelu(x):
    return jax.nn.gelu(x, approximate=True)

def _silu(x):
    return jax.nn.silu(x)

def _sigmoid(x):
    return jax.nn.sigmoid(x)

def _layernorm(x, axis=-1, eps=1e-05):
    m = jnp.mean(x, axis=axis, keepdims=True)
    v = jnp.var(x, axis=axis, keepdims=True)
    return (x - m) / jnp.sqrt(v + eps)

def _scatter_add(tgt, idx, src, axis=0):
    return tgt.at[idx].add(src)

def _segment_sum(src, seg, n):
    return jax.ops.segment_sum(src, seg, n)
kernel_name = 'mk_gps_d1_gnn_r32_32dc75'

def setup_inputs(seed: int=0):
    np.random.seed(seed)
    _w = jnp.asarray

    def _rec_inputs():
        import jax
        import jax.numpy as jnp
        _gk = jax.random.key(seed)
        x = -0.0005963 + 1.001 * jax.random.normal(jax.random.fold_in(_gk, 1), (96, 1024), jnp.float32)
        src = jax.random.randint(jax.random.fold_in(_gk, 2), (3072,), 0, 96, jnp.int32)
        dst = jax.random.randint(jax.random.fold_in(_gk, 3), (3072,), 0, 96, jnp.int32)
        _o = jnp.argsort(dst, stable=True)
        src = src[_o]
        dst = dst[_o]
        edge_type_5 = jax.random.randint(jax.random.fold_in(_gk, 12), (3072,), 0, 5, jnp.int32)
        return (x, src, dst, edge_type_5)
    x, src, dst, edge_type_5 = _rec_inputs()

    def _L0_gnn_setup():
        import jax, jax.numpy as jnp
        import numpy as np
        N = 96
        E = 3072
        IN_F = 1024
        OUT_F = 1024
        H = 16
        D = OUT_F // H
        NUM_ETYPES = 4

        def _build_mask(edge_index, edge_type, edge_type_weights, dtype):
            src, dst = (edge_index[0], edge_index[1])
            w = jax.nn.softplus(edge_type_weights)
            mask = jnp.full((N, N), -jnp.inf, dtype=dtype)
            mask = mask.at[src, dst].set(w[edge_type - 1])
            diag = jnp.diagonal(mask)
            idx = jnp.arange(N)
            mask = mask.at[idx, idx].set(jnp.where(jnp.isneginf(diag), w[3], diag))
            return mask
        key = jax.random.key(seed)
        ks = jax.random.split(key, 20)
        p = lambda k, shape: jax.random.normal(k, shape, dtype=jnp.float32) * 0.02
        return {'x': jax.random.normal(ks[0], (N, IN_F), dtype=jnp.float32), 'edge_index': jax.random.randint(ks[1], (2, E), 0, N), 'edge_type': jax.random.randint(ks[2], (E,), 1, NUM_ETYPES + 1), 'edge_type_weights': jnp.ones((NUM_ETYPES,), jnp.float32) + 0.1 * jax.random.normal(ks[3], (NUM_ETYPES,), dtype=jnp.float32), 'wq': p(ks[4], (OUT_F, IN_F)), 'bq': p(ks[5], (OUT_F,)), 'wk': p(ks[6], (OUT_F, IN_F)), 'bk': p(ks[7], (OUT_F,)), 'wv': p(ks[8], (OUT_F, IN_F)), 'bv': p(ks[9], (OUT_F,)), 'wiq': p(ks[10], (OUT_F, OUT_F)), 'biq': p(ks[11], (OUT_F,)), 'wik': p(ks[12], (OUT_F, OUT_F)), 'bik': p(ks[13], (OUT_F,)), 'wiv': p(ks[14], (OUT_F, OUT_F)), 'biv': p(ks[15], (OUT_F,)), 'wo': p(ks[16], (OUT_F, OUT_F)), 'bo': p(ks[17], (OUT_F,))}
    _L0_gnn_all = _L0_gnn_setup()
    _L0_gnn_in = {k: v for k, v in _L0_gnn_all.items() if k in ('edge_type_weights', 'wq', 'bq', 'wk', 'bk', 'wv', 'bv', 'wiq', 'biq', 'wik', 'bik', 'wiv', 'biv', 'wo', 'bo')}
    del _L0_gnn_all

    def _L0_mix_setup():
        import jax, jax.numpy as jnp
        import numpy as np
        D_MODEL = 1024
        N_HEAD = 16
        HEAD_D = D_MODEL // N_HEAD
        D_FF = 128
        LN_EPS = 1e-05
        ATTN_EPS = 1e-06

        def _layer_norm(x, g, b, eps=LN_EPS):
            mu = jnp.mean(x, axis=-1, keepdims=True)
            var = jnp.var(x, axis=-1, keepdims=True)
            return (x - mu) * jax.lax.rsqrt(var + eps) * g + b

        def _linear_attention(x, qkv_w, qkv_b, out_w, out_b):
            B, N, C = x.shape
            qkv = (x @ qkv_w + qkv_b).reshape(B, N, 3, N_HEAD, HEAD_D)
            qkv = jnp.transpose(qkv, (2, 0, 3, 1, 4))
            q, k, v = (qkv[0], qkv[1], qkv[2])
            qf = jax.nn.elu(q) + 1.0
            kf = jax.nn.elu(k) + 1.0
            kv = jnp.einsum('bhnd,bhne->bhde', kf.astype(jnp.float32), v.astype(jnp.float32)).astype(v.dtype)
            y_num = jnp.einsum('bhnd,bhde->bhne', qf, kv)
            z = jnp.sum(kf.astype(jnp.float32), axis=2)
            y_den = jnp.einsum('bhnd,bhd->bhn', qf, z.astype(qf.dtype))
            y_den = jnp.maximum(y_den, ATTN_EPS)[..., None]
            y = (y_num / y_den).transpose(0, 2, 1, 3).reshape(B, N, C)
            return y @ out_w + out_b
        key = jax.random.key(seed)
        ks = jax.random.split(key, 16)
        s = 0.02
        return {'src': jax.random.normal(ks[0], (4, 128, D_MODEL), dtype=jnp.float32), 'qkv_w': jax.random.normal(ks[1], (D_MODEL, 3 * D_MODEL), dtype=jnp.float32) * s, 'qkv_b': jax.random.normal(ks[2], (3 * D_MODEL,), dtype=jnp.float32) * s, 'out_w': jax.random.normal(ks[3], (D_MODEL, D_MODEL), dtype=jnp.float32) * s, 'out_b': jax.random.normal(ks[4], (D_MODEL,), dtype=jnp.float32) * s, 'w1': jax.random.normal(ks[5], (D_MODEL, D_FF), dtype=jnp.float32) * s, 'b1': jax.random.normal(ks[6], (D_FF,), dtype=jnp.float32) * s, 'w2': jax.random.normal(ks[7], (D_FF, D_MODEL), dtype=jnp.float32) * s, 'b2': jax.random.normal(ks[8], (D_MODEL,), dtype=jnp.float32) * s, 'g1': jnp.ones((D_MODEL,), dtype=jnp.float32), 'be1': jnp.zeros((D_MODEL,), dtype=jnp.float32), 'g2': jnp.ones((D_MODEL,), dtype=jnp.float32), 'be2': jnp.zeros((D_MODEL,), dtype=jnp.float32)}
    _L0_mix_all = _L0_mix_setup()
    _L0_mix_in = {k: v for k, v in _L0_mix_all.items() if k in ('qkv_w', 'qkv_b', 'out_w', 'out_b', 'w1', 'b1', 'w2', 'b2', 'g1', 'be1', 'g2', 'be2')}
    del _L0_mix_all

    def _L0_ffn_setup():
        import jax, jax.numpy as jnp
        import numpy as np
        INT8_MAX = 127.0

        def _absmax_scale(x, axes):
            amax = jnp.max(jnp.abs(x), axis=axes, keepdims=True)
            return jnp.maximum(amax, 1e-12) / INT8_MAX
        key = jax.random.key(seed)
        k1, k2 = jax.random.split(key)
        lhs = jax.random.normal(k1, (4, 256, 1024), dtype=jnp.float32)
        rhs = jax.random.normal(k2, (1024, 1024), dtype=jnp.float32)
        return {'lhs': lhs, 'rhs': rhs}
    _L0_ffn_all = _L0_ffn_setup()
    _L0_ffn_in = {k: v for k, v in _L0_ffn_all.items() if k in ('rhs',)}
    del _L0_ffn_all
    return {'x': x, 'src': src, 'dst': dst, 'edge_type_5': edge_type_5, 'L0_gnn_edge_type_weights': _L0_gnn_in['edge_type_weights'], 'L0_gnn_wq': _L0_gnn_in['wq'], 'L0_gnn_bq': _L0_gnn_in['bq'], 'L0_gnn_wk': _L0_gnn_in['wk'], 'L0_gnn_bk': _L0_gnn_in['bk'], 'L0_gnn_wv': _L0_gnn_in['wv'], 'L0_gnn_bv': _L0_gnn_in['bv'], 'L0_gnn_wiq': _L0_gnn_in['wiq'], 'L0_gnn_biq': _L0_gnn_in['biq'], 'L0_gnn_wik': _L0_gnn_in['wik'], 'L0_gnn_bik': _L0_gnn_in['bik'], 'L0_gnn_wiv': _L0_gnn_in['wiv'], 'L0_gnn_biv': _L0_gnn_in['biv'], 'L0_gnn_wo': _L0_gnn_in['wo'], 'L0_gnn_bo': _L0_gnn_in['bo'], 'L0_mix_qkv_w': _L0_mix_in['qkv_w'], 'L0_mix_qkv_b': _L0_mix_in['qkv_b'], 'L0_mix_out_w': _L0_mix_in['out_w'], 'L0_mix_out_b': _L0_mix_in['out_b'], 'L0_mix_w1': _L0_mix_in['w1'], 'L0_mix_b1': _L0_mix_in['b1'], 'L0_mix_w2': _L0_mix_in['w2'], 'L0_mix_b2': _L0_mix_in['b2'], 'L0_mix_g1': _L0_mix_in['g1'], 'L0_mix_be1': _L0_mix_in['be1'], 'L0_mix_g2': _L0_mix_in['g2'], 'L0_mix_be2': _L0_mix_in['be2'], 'L0_ffn_rhs': _L0_ffn_in['rhs']}

def reference(x, src, dst, edge_type_5, L0_gnn_edge_type_weights, L0_gnn_wq, L0_gnn_bq, L0_gnn_wk, L0_gnn_bk, L0_gnn_wv, L0_gnn_bv, L0_gnn_wiq, L0_gnn_biq, L0_gnn_wik, L0_gnn_bik, L0_gnn_wiv, L0_gnn_biv, L0_gnn_wo, L0_gnn_bo, L0_mix_qkv_w, L0_mix_qkv_b, L0_mix_out_w, L0_mix_out_b, L0_mix_w1, L0_mix_b1, L0_mix_w2, L0_mix_b2, L0_mix_g1, L0_mix_be1, L0_mix_g2, L0_mix_be2, L0_ffn_rhs):
    import jax
    import jax.numpy as jnp

    def _L0_gnn_ref(x, edge_index, edge_type, edge_type_weights, wq, bq, wk, bk, wv, bv, wiq, biq, wik, bik, wiv, biv, wo, bo):
        import jax, jax.numpy as jnp
        import numpy as np
        N = 96
        E = 3072
        IN_F = 1024
        OUT_F = 1024
        H = 16
        D = OUT_F // H
        NUM_ETYPES = 4

        def _build_mask(edge_index, edge_type, edge_type_weights, dtype):
            src, dst = (edge_index[0], edge_index[1])
            w = jax.nn.softplus(edge_type_weights)
            mask = jnp.full((N, N), -jnp.inf, dtype=dtype)
            mask = mask.at[src, dst].set(w[edge_type - 1])
            diag = jnp.diagonal(mask)
            idx = jnp.arange(N)
            mask = mask.at[idx, idx].set(jnp.where(jnp.isneginf(diag), w[3], diag))
            return mask
        q = x @ wq.T + bq
        k = x @ wk.T + bk
        v = x @ wv.T + bv
        q2 = (q @ wiq.T + biq).reshape(N, H, D).transpose(1, 0, 2)
        k2 = (k @ wik.T + bik).reshape(N, H, D).transpose(1, 0, 2)
        v2 = (v @ wiv.T + biv).reshape(N, H, D).transpose(1, 0, 2)
        mask = _build_mask(edge_index, edge_type, edge_type_weights, x.dtype)
        scale = 1.0 / np.sqrt(D).astype(np.float32)
        scores = jnp.einsum('hnd,hmd->hnm', q2, k2) * scale + mask[None]
        attn = jax.nn.softmax(scores, axis=-1)
        out = jnp.einsum('hnm,hmd->hnd', attn, v2)
        out = out.transpose(1, 0, 2).reshape(N, OUT_F)
        return out @ wo.T + bo

    def _L0_mix_ref(src, qkv_w, qkv_b, out_w, out_b, w1, b1, w2, b2, g1, be1, g2, be2):
        import jax, jax.numpy as jnp
        import numpy as np
        D_MODEL = 1024
        N_HEAD = 16
        HEAD_D = D_MODEL // N_HEAD
        D_FF = 128
        LN_EPS = 1e-05
        ATTN_EPS = 1e-06

        def _layer_norm(x, g, b, eps=LN_EPS):
            mu = jnp.mean(x, axis=-1, keepdims=True)
            var = jnp.var(x, axis=-1, keepdims=True)
            return (x - mu) * jax.lax.rsqrt(var + eps) * g + b

        def _linear_attention(x, qkv_w, qkv_b, out_w, out_b):
            B, N, C = x.shape
            qkv = (x @ qkv_w + qkv_b).reshape(B, N, 3, N_HEAD, HEAD_D)
            qkv = jnp.transpose(qkv, (2, 0, 3, 1, 4))
            q, k, v = (qkv[0], qkv[1], qkv[2])
            qf = jax.nn.elu(q) + 1.0
            kf = jax.nn.elu(k) + 1.0
            kv = jnp.einsum('bhnd,bhne->bhde', kf.astype(jnp.float32), v.astype(jnp.float32)).astype(v.dtype)
            y_num = jnp.einsum('bhnd,bhde->bhne', qf, kv)
            z = jnp.sum(kf.astype(jnp.float32), axis=2)
            y_den = jnp.einsum('bhnd,bhd->bhn', qf, z.astype(qf.dtype))
            y_den = jnp.maximum(y_den, ATTN_EPS)[..., None]
            y = (y_num / y_den).transpose(0, 2, 1, 3).reshape(B, N, C)
            return y @ out_w + out_b
        attn_out = _linear_attention(_layer_norm(src, g1, be1), qkv_w, qkv_b, out_w, out_b)
        x = src + attn_out
        h = jax.nn.gelu(_layer_norm(x, g2, be2) @ w1 + b1, approximate=False)
        return x + h @ w2 + b2

    def _L0_ffn_ref(lhs, rhs):
        import jax, jax.numpy as jnp
        import numpy as np
        INT8_MAX = 127.0

        def _absmax_scale(x, axes):
            amax = jnp.max(jnp.abs(x), axis=axes, keepdims=True)
            return jnp.maximum(amax, 1e-12) / INT8_MAX
        lhs_scale = _absmax_scale(lhs, (2,))
        rhs_scale = _absmax_scale(rhs, (0,))
        q_lhs = jnp.clip(jnp.round(lhs / lhs_scale), -INT8_MAX, INT8_MAX).astype(jnp.int8)
        q_rhs = jnp.clip(jnp.round(rhs / rhs_scale), -INT8_MAX, INT8_MAX).astype(jnp.int8)
        acc = jax.lax.dot_general(q_lhs, q_rhs, (((2,), (0,)), ((), ())), preferred_element_type=jnp.int32)
        return acc.astype(jnp.float32) * lhs_scale * rhs_scale
    edge_index = jnp.stack([src, dst])
    xn = _layernorm(x, axis=-1)
    x = x + _L0_gnn_ref(xn, edge_index, edge_type_5, L0_gnn_edge_type_weights, L0_gnn_wq, L0_gnn_bq, L0_gnn_wk, L0_gnn_bk, L0_gnn_wv, L0_gnn_bv, L0_gnn_wiq, L0_gnn_biq, L0_gnn_wik, L0_gnn_bik, L0_gnn_wiv, L0_gnn_biv, L0_gnn_wo, L0_gnn_bo) + _L0_mix_ref(xn[None], L0_mix_qkv_w, L0_mix_qkv_b, L0_mix_out_w, L0_mix_out_b, L0_mix_w1, L0_mix_b1, L0_mix_w2, L0_mix_b2, L0_mix_g1, L0_mix_be1, L0_mix_g2, L0_mix_be2)[0]
    x = x + _L0_ffn_ref(_layernorm(x, axis=-1)[None], L0_ffn_rhs)[0]
    return x

_drawn_inputs = setup_inputs


def setup_inputs(seed=0):
    import zlib

    import numpy as np

    out = dict(_drawn_inputs(seed))
    spreads = {'L0_mix_g1': (1.0, 0.6),
     'L0_mix_be1': (0.0, 0.361),
     'L0_mix_g2': (1.0, 0.6),
     'L0_mix_be2': (0.0, 0.8)}
    factors = {'L0_gnn_edge_type_weights': 196.525,
     'L0_gnn_wq': 7.035,
     'L0_gnn_bq': 8.0,
     'L0_gnn_wk': 7.047,
     'L0_gnn_bk': 200.0,
     'L0_gnn_bv': 7.211,
     'L0_gnn_wiq': 7.08,
     'L0_gnn_biq': 37.366,
     'L0_gnn_wik': 7.041,
     'L0_gnn_bik': 200.0,
     'L0_gnn_biv': 5.843,
     'L0_gnn_bo': 4.548,
     'L0_mix_qkv_b': 5.666,
     'L0_mix_out_b': 4.497,
     'L0_mix_b1': 29.374,
     'L0_mix_b2': 4.589}
    for name, (base, spread) in spreads.items():
        noise = np.random.default_rng([zlib.crc32(name.encode()), seed]).standard_normal(out[name].shape)
        drawn = base * np.exp(spread * noise) if base else spread * noise
        out[name] = jnp.asarray(drawn.astype(out[name].dtype))
    for name, factor in factors.items():
        out[name] = (out[name] * factor).astype(out[name].dtype)
    return out
```

```python
from contextlib import ExitStack

import concourse.bass as bass
from concourse import mybir

F32 = mybir.dt.float32
BF16 = mybir.dt.bfloat16
I32 = mybir.dt.int32
ALU = mybir.AluOpType
ACT = mybir.ActivationFunctionType
AX = mybir.AxisListType

P = 128
N = 96
D = 1024
KT = D // P
H = 16
HD = D // H
E = 3072
EC = E // P
HALF = 512
TPB = KT // 2
LN_EPS = 1e-5
ATTN_EPS = 1e-6
ABSMAX_FLOOR = 1e-12
INT8_MAX = 127.0
ROUND = 1.5 * 2.0 ** 23
FAR = 1e30
DIGIT = 4
DIGIT0 = 80

ORDER = ["q", "mk", "mv", "k", "mq", "v", "q2", "ow", "k2", "w12", "v2", "wo"]
CHUNK = 2 * D
RING = 9
FIRST = {}
_n = 0
for _w in ORDER:
    FIRST[_w] = _n
    _n += 1 if _w == "w12" else 4
CHUNKS = _n

COLS = ["bq", "bk", "bv", "biq", "bik", "biv", "mqb", "mkb", "mvb", "outb", "g1", "be1", "g2", "be2"]
COL = {name: KT * i for i, name in enumerate(COLS)}
COL_B1 = KT * len(COLS)
NCOLS = COL_B1 + 1


def build(nc, x, weights, rhs, cols, rowbias, edge_cols, edge_rows, etw, out):
    assert CHUNKS % RING == 0
    with ExitStack() as ctx:
        sems = {}

        def ev(name):
            if name not in sems:
                sems[name] = ctx.enter_context(nc.semaphore(name))
            return sems[name]

        def sb(name, shape, dt=F32):
            return ctx.enter_context(nc.sbuf_tensor(name, shape, dt))

        ring = sb("ring", [P, RING, CHUNK])
        rhs_stage = sb("rhs_stage", [P, 2, CHUNK])
        rhs_q = sb("rhs_q", [P, 4, CHUNK], BF16)
        x_rows = sb("x_rows", [N, D])
        xn_rows = sb("xn_rows", [N, D])
        ln_rows = sb("ln_rows", [N, D])
        base_rows = sb("base_rows", [N, D])
        xnT = sb("xnT", [P, KT, N])
        lnT = sb("lnT", [P, KT, N])
        qT = sb("qT", [P, KT, N])
        kT = sb("kT", [P, KT, N])
        vT = sb("vT", [P, KT, N])
        mqT = sb("mqT", [P, KT, N])
        mkT = sb("mkT", [P, KT, N])
        mvT = sb("mvT", [P, KT, N])
        negT = sb("negT", [P, KT, N])
        expT = sb("expT", [P, KT, N])
        kf_rows = sb("kf_rows", [N, D])
        mv_rows = sb("mv_rows", [N, D])
        kvz = sb("kvz", [P, 2, KT, P])
        yT = sb("yT", [P, KT, N])
        late = sb("late", [P, E // 2 + EC * N // 2])
        cols_sb = sb("cols_sb", [P, NCOLS])
        rowb = sb("rowb", [2, D])
        hT = sb("hT", [P, N])
        ident = sb("ident", [P, P])
        identb = sb("identb", [P, P], BF16)
        upper = sb("upper", [P, P])
        blockm = sb("blockm", [P, P])
        ones = sb("ones", [P, P])
        keyw = sb("keyw", [2, P], BF16)
        node_iota = sb("node_iota", [P, N])
        digit_exp = sb("digit_exp", [P, EC], I32)
        digit = sb("digit", [P, EC], I32)
        edge_i = sb("edge_i", [P, 3, EC], I32)
        edge_f = sb("edge_f", [P, 3, EC])
        keyc = sb("keyc", [P, EC])
        dup = sb("dup", [P, EC])
        code = sb("code", [P, EC])
        is0 = sb("is0", [P, EC])
        junk = sb("junk", [P, P])
        dst_val = sb("dst_val", [P, EC, N], BF16)
        etw_sb = sb("etw_sb", [N, 4])
        sp_a = sb("sp_a", [N, 4])
        sp_b = sb("sp_b", [N, 4])
        wmask = sb("wmask", [N, 4])
        ediag = sb("ediag", [N, N])
        far = sb("far", [N, N])
        esum = sb("esum", [N, N])
        ecode = sb("ecode", [N, N], I32)
        ecodef = sb("ecodef", [N, N])
        absent = sb("absent", [N, N])
        mask = sb("mask", [N, N])
        mtmp = sb("mtmp", [N, N])
        z_sb = sb("z_sb", [P, KT])
        stats = sb("stats", [N, 4, 2, 6])
        mv = sb("mv", [N, 4, 2])
        sd = sb("sd", [N, 4])
        rstd = sb("rstd", [N, 4])
        smax = sb("smax", [N, H])
        ssum = sb("ssum", [N, H])
        rsum = sb("rsum", [N, H])
        lscale = sb("lscale", [N, 4])
        ramax = sb("ramax", [P, 2, 256])
        rinv = sb("rinv", [P, 2, 256])
        rscale = sb("rscale", [P, D])
        q8T = sb("q8T", [P, KT, N], BF16)
        eps = sb("eps", [N, 1])

        y1T, owT = xnT, expT
        q2T, k2T, v2T, aT = mqT, mkT, mvT, vT
        y1_rows = kf_rows
        ln2_rows, ln2T = mv_rows, lnT
        probs = kvz[:, :, :, :].rearrange("p a b c -> p (a b c)")[0:N, 0:H * N].rearrange("p (h n) -> p h n", h=H)
        x1_rows, xl_rows = xn_rows, ln_rows
        q_rows = mv_rows[:, 0:D // 2].bitcast(BF16)
        probsT = late[0:N, 0:H * N].rearrange("p (h n) -> p h n", h=H)
        v2_rows = late[0:N, H * N:H * N + D]
        keyrow = late[0:2, 0:E // 2].bitcast(BF16)
        src_hot = late[:, E // 2:E // 2 + EC * N // 2].bitcast(BF16).rearrange("p (c n) -> p c n", c=EC)
        edge_row_i = rhs_q[:, :, :].rearrange("p a b -> p (a b)")[0:2, 0:2 * E].bitcast(I32)

        bank = [ctx.enter_context(nc.psum_tensor(f"bank{i}", [P, HALF], F32)) for i in range(8)]

        def slot(w, q):
            return ring[:, (FIRST[w] + q) % RING, :]

        def chunk_count(w, q):
            return FIRST[w] + q + 1

        def tiles(b):
            return bank[b][:, 0:TPB * N].rearrange("p (j n) -> p j n", j=TPB)

        def col(name, j0, j1):
            return cols_sb[:, COL[name] + j0:COL[name] + j1]

        def spread(ap, n):
            return ap.unsqueeze(2).to_broadcast([ap.shape[0], ap.shape[1], n])

        def score_bank(h):
            return [0, 1, 6, 7][2 * (h // 8) + h % 2], (h % 8) // 2

        def group_heads(g):
            return range(8 * (g // 2) + g % 2, 8 * (g // 2) + 8, 2)

        block = ctx.enter_context(nc.Block())

        @block.sync
        def _(sp):
            for s in range(RING):
                sp.dma_start(ring[:, s, :], weights[s]).then_inc(ev(f"slot_full{s}"), 16)
            with sp.Fori(1, CHUNKS // RING) as r:
                for s in range(RING):
                    sp.wait_ge(ev("chunk_done"), r * RING + (s + 1 - RING))
                    sp.dma_start(ring[:, s, :], weights[bass.ds(r * RING + s, 1)].rearrange("a p n -> (a p) n"))\
                        .then_inc(ev(f"slot_full{s}"), 16)
            for h in range(2):
                sp.wait_ge(ev("out_ready"), h + 1)
                sp.dma_start(out[:, h * HALF:(h + 1) * HALF], x1_rows[:, h * HALF:(h + 1) * HALF])\
                    .then_inc(ev("out_stored"), 16)
            sp.wait_ge(ev("out_stored"), 32)

        @block.gpsimd
        def _(pool):
            for c in range(2):
                pool.dma_start(rhs_stage[:, c, :], rhs[c]).then_inc(ev(f"rhs_full{c}"), 16)
            pool.memset(ident[:, :], 0.0).then_inc(ev("zeros"), 1)
            pool.memset(identb[:, :], 0.0).then_inc(ev("zeros"), 1)
            pool.memset(upper[:, :], 1.0).then_inc(ev("zeros"), 1)
            pool.wait_ge(ev("zeros"), 3)
            pool.affine_select(out=ident[:, :], in_=ident[:, :], compare_op=ALU.not_equal, fill=1.0, base=0,
                               pattern=[[-1, P]], channel_multiplier=1).then_inc(ev("ident"), 1)
            pool.affine_select(out=identb[:, :], in_=identb[:, :], compare_op=ALU.not_equal, fill=1.0, base=0,
                               pattern=[[-1, P]], channel_multiplier=1).then_inc(ev("identb"), 1)
            pool.affine_select(out=upper[:, :], in_=upper[:, :], compare_op=ALU.is_ge, fill=0.0, base=-1,
                               pattern=[[1, P]], channel_multiplier=-1).then_inc(ev("upper"), 1)
            pool.iota(node_iota[:, :], [[1, N]], base=0, channel_multiplier=0,
                      allow_small_or_imprecise_dtypes=True).then_inc(ev("node_iota"), 1)
            pool.iota(digit_exp[:, :], [[DIGIT, EC]], base=DIGIT0, channel_multiplier=0).then_inc(ev("digit_exp"), 1)

            pool.wait_ge(ev("x_loaded"), 16)
            pool.wait_ge(ev("rowbias_out"), 2)
            pool.tensor_tensor(base_rows[:, :], x_rows[:, :], base_rows[:, :], ALU.add).then_inc(ev("base0"), 1)

            for c in range(4):
                pool.wait_ge(ev("rhs_pmax"), c + 1)
                pool.partition_all_reduce(ramax[:, c % 2, :], ramax[:, c % 2, :], P,
                                          bass.bass_isa.ReduceOp.max).then_inc(ev("rhs_amax"), 1)
                if c + 2 < 4:
                    pool.wait_ge(ev("rhs_rounded"), c + 1)
                    pool.dma_start(rhs_stage[:, c % 2, :], rhs[c + 2]).then_inc(ev(f"rhs_full{c % 2}"), 16)

            pool.wait_ge(ev("base0"), 1)
            pool.wait_ge(ev("y1_rows"), 2)
            pool.tensor_tensor(base_rows[:, :], base_rows[:, :], y1_rows[:, :], ALU.add).then_inc(ev("base"), 1)

        @block.scalar
        def _(act):
            act.dma_start(x_rows[:, :], x).then_inc(ev("x_loaded"), 16)
            act.dma_start(cols_sb[:, :], cols).then_inc(ev("cols_loaded"), 16)
            act.dma_start(rowb[:, :], rowbias).then_inc(ev("rowb_loaded"), 16)
            act.dma_start(edge_i[:, :, :], edge_cols).then_inc(ev("edge_cols_loaded"), 16)
            act.dma_start(edge_row_i, edge_rows).then_inc(ev("edge_rows_loaded"), 16)
            act.dma_start(etw_sb[:, :], etw).then_inc(ev("etw_loaded"), 16)

            def deviation(i):
                act.wait_ge(ev("ln_stats"), i + 1)
                nc.scalar.activation(sd[:, i:i + 1], mv[:, i, 1:2], ACT.Sqrt, bias=eps[:, :]).then_inc(ev("ln_sd"), 1)

            def drain_T(w, banks, dst, bias, name):
                for h in range(2):
                    act.wait_ge(ev("chunk_done"), chunk_count(w, 2 * h + 1))
                    for j in range(TPB * h, TPB * h + TPB):
                        ins = nc.scalar.activation(dst[:, j, :], tiles(banks[h])[:, j % TPB, :], ACT.Identity,
                                                   bias=col(bias, j, j + 1))
                    ins.then_inc(ev(name), 1)

            def copy_half(dst, src, name):
                nc.scalar.activation(dst, src, ACT.Copy).then_inc(ev(name), 1)

            act.wait_ge(ev("eps_set"), 1)
            deviation(0)
            act.wait_ge(ev("rowbias_ps"), 2)
            for h in range(2):
                copy_half(base_rows[:, h * HALF:(h + 1) * HALF], bank[6 + h][0:N, :], "rowbias_out")
            deviation(1)
            act.wait_ge(ev("etw_loaded"), 16)
            nc.scalar.activation(sp_a[:, :], etw_sb[:, :], ACT.Abs).then_inc(ev("etw_abs"), 1)
            act.wait_ge(ev("etw_abs"), 1)
            nc.scalar.activation(sp_b[:, :], sp_a[:, :], ACT.Exp, scale=-1.0).then_inc(ev("etw_exp"), 1)
            act.wait_ge(ev("etw_exp"), 1)
            nc.scalar.activation(sp_a[:, :], sp_b[:, :], ACT.Ln, bias=1.0).then_inc(ev("etw_ln"), 1)
            act.wait_ge(ev("cols_loaded"), 16)
            drain_T("q", (2, 3), qT, "bq", "qT")
            drain_T("mk", (0, 1), mkT, "mkb", "mkT")
            act.wait_ge(ev("mk_neg"), 1)
            nc.scalar.activation(expT[:, :, :], negT[:, :, :], ACT.Exp).then_inc(ev("mk_exp"), 1)
            drain_T("mv", (2, 3), mvT, "mvb", "mvT")
            act.wait_ge(ev("kf_tr"), 2)
            for h in range(2):
                copy_half(kf_rows[:, h * HALF:(h + 1) * HALF], bank[4 + h][0:N, :], "kf_rows")
            act.wait_ge(ev("mv_tr"), 2)
            for h in range(2):
                copy_half(mv_rows[:, h * HALF:(h + 1) * HALF], bank[6 + h][0:N, :], "mv_rows")
            drain_T("k", (0, 1), kT, "bk", "kT")
            drain_T("mq", (2, 3), mqT, "mqb", "mqT")
            act.wait_ge(ev("mq_neg"), 1)
            nc.scalar.activation(expT[:, :, :], negT[:, :, :], ACT.Exp).then_inc(ev("mq_exp"), 1)
            drain_T("v", (0, 1), vT, "bv", "vT")

            def round_rhs(c):
                act.wait_ge(ev("rhs_scaled"), c + 1)
                st = rhs_stage[:, c % 2, :]
                nc.scalar.activation(st, st, ACT.Copy, bias=ROUND).then_inc(ev("rhs_magic"), 1)
                act.wait_ge(ev("rhs_magic"), c + 1)
                nc.scalar.activation(rhs_q[:, c, :], st, ACT.Copy, bias=-ROUND).then_inc(ev("rhs_rounded"), 1)

            round_rhs(0)
            act.wait_ge(ev("num_ps"), 1)
            drain_T("q2", (2, 3), q2T, "biq", "q2T")
            round_rhs(1)
            drain_T("ow", (0, 1), owT, "outb", "owT")
            act.wait_ge(ev("y1_tr"), 2)
            for h in range(2):
                copy_half(y1_rows[:, h * HALF:(h + 1) * HALF], bank[4 + h][0:N, :], "y1_rows")
            deviation(2)
            drain_T("k2", (2, 3), k2T, "bik", "k2T")
            round_rhs(2)
            round_rhs(3)
            act.wait_ge(ev("h_ps"), 1)
            nc.scalar.activation(hT[:, :], bank[4][:, 0:N], ACT.Gelu, bias=cols_sb[:, COL_B1:COL_B1 + 1])\
                .then_inc(ev("hT"), 1)
            for g in range(4):
                act.wait_ge(ev("scores_shifted"), g + 1)
                hs = group_heads(g)
                pg = probs[:, hs[0]:hs[-1] + 1:2, :]
                nc.scalar.activation(pg, pg, ACT.Exp).then_inc(ev("probs_exp"), 1)
            for h in range(2):
                act.wait_ge(ev("chunk_done"), chunk_count("v2", 2 * h + 1))
                nc.scalar.activation(v2T[:, TPB * h:TPB * (h + 1), :], tiles(2 + h), ACT.Copy).then_inc(ev("v2T"), 1)
            act.wait_ge(ev("v2_tr"), 2)
            for h in range(2):
                copy_half(v2_rows[:, h * HALF:(h + 1) * HALF], bank[h][0:N, :], "v2_rows")
            for h in range(2):
                act.wait_ge(ev("pv_ps"), h + 1)
                for j in range(TPB * h, TPB * h + TPB):
                    ins = nc.scalar.activation(aT[:, j, :], tiles(2 + h)[:, j % TPB, :], ACT.Identity,
                                               bias=col("biv", j, j + 1))
                ins.then_inc(ev("aT"), 1)
            deviation(3)

        @block.vector
        def _(dve):
            V = nc.vector

            def layer_norm(i, src, dst, src_ready):
                for h in range(2):
                    dve.wait_ge(ev(src_ready[0]), src_ready[1 + h])
                    V.bn_stats(stats[:, i, h, :], src[:, h * HALF:(h + 1) * HALF]).then_inc(ev("bn"), 1)
                dve.wait_ge(ev("bn"), 2 * i + 2)
                V.bn_aggr(mv[:, i, :], stats[:, i, :, :]).then_inc(ev("ln_stats"), 1)
                dve.wait_ge(ev("ln_sd"), i + 1)
                V.reciprocal(rstd[:, i:i + 1], sd[:, i:i + 1]).then_inc(ev("ln_rstd"), 1)
                dve.wait_ge(ev("ln_rstd"), i + 1)
                V.tensor_scalar(dst, src, mv[:, i, 0:1], rstd[:, i:i + 1], ALU.subtract, ALU.mult)\
                    .then_inc(ev("ln_done"), 1)

            def affine_T(banks, dst, g, b, ps_ready, name):
                for h in range(2):
                    js = slice(TPB * h, TPB * (h + 1))
                    dve.wait_ge(ev(ps_ready), h + 1)
                    V.tensor_tensor(dst[:, js, :], tiles(banks[h]), spread(col(g, js.start, js.stop), N), ALU.mult)\
                        .then_inc(ev(name + "_g"), 1)
                    dve.wait_ge(ev(name + "_g"), h + 1)
                    V.tensor_tensor(dst[:, js, :], dst[:, js, :], spread(col(b, js.start, js.stop), N), ALU.add)\
                        .then_inc(ev(name), 1)

            def features(src, neg, exp, ready, name):
                dve.wait_ge(ev(ready), 2)
                V.tensor_scalar(neg[:, :, :], src[:, :, :], 0.0, None, ALU.min).then_inc(ev(name + "_neg"), 1)
                dve.wait_ge(ev(name + "_exp"), 1)
                V.scalar_tensor_tensor(src[:, :, :], src[:, :, :], 0.0, exp[:, :, :], ALU.max, ALU.add)\
                    .then_inc(ev(name + "_feat"), 1)

            V.memset(eps[:, :], LN_EPS).then_inc(ev("eps_set"), 1)
            V.memset(ones[:, :], 1.0).then_inc(ev("ones"), 1)
            V.memset(keyw[:, :], 1.0).then_inc(ev("keyw0"), 1)
            dve.wait_ge(ev("keyw0"), 1)
            V.memset(keyw[0:1, :], float(P)).then_inc(ev("keyw"), 1)
            V.memset(blockm[:, :], 0.0).then_inc(ev("blockm0"), 1)
            dve.wait_ge(ev("blockm0"), 1)
            V.memset(blockm[0:HD, 0:HD], 1.0).then_inc(ev("blockm"), 1)
            V.memset(blockm[HD:P, HD:P], 1.0).then_inc(ev("blockm"), 1)

            layer_norm(0, x_rows[:, :], xn_rows[:, :], ("x_loaded", 16, 16))
            for h in range(2):
                dve.wait_ge(ev("xn_tr"), h + 1)
                V.tensor_copy(xnT[:, TPB * h:TPB * (h + 1), :], tiles(h)).then_inc(ev("xnT"), 1)
            layer_norm(1, xn_rows[:, :], ln_rows[:, :], ("ln_done", 1, 1))
            dve.wait_ge(ev("cols_loaded"), 16)
            affine_T((4, 5), lnT, "g1", "be1", "lnx_tr", "lnT")

            dve.wait_ge(ev("edge_rows_loaded"), 16)
            V.tensor_copy(keyrow, edge_row_i).then_inc(ev("keyrow"), 1)
            dve.wait_ge(ev("edge_cols_loaded"), 16)
            V.tensor_copy(edge_f[:, :, :], edge_i[:, :, :]).then_inc(ev("edge_f"), 1)
            dve.wait_ge(ev("edge_f"), 1)
            esrc, edst, etype = (edge_f[:, i, :] for i in range(3))
            V.scalar_tensor_tensor(keyc[:, :], esrc, float(P), edst, ALU.mult, ALU.add).then_inc(ev("keyc"), 1)
            V.tensor_scalar(is0[:, :], etype, 0.0, 4.0, ALU.is_equal, ALU.mult).then_inc(ev("is0"), 1)
            dve.wait_ge(ev("digit_exp"), 1)
            V.tensor_scalar(digit[:, :], digit_exp[:, :], 23, None, ALU.logical_shift_left).then_inc(ev("digit"), 1)
            dve.wait_ge(ev("is0"), 1)
            V.tensor_tensor(code[:, :], etype, is0[:, :], ALU.add).then_inc(ev("code"), 1)
            dve.wait_ge(ev("code"), 1)
            dve.wait_ge(ev("digit"), 1)
            V.tensor_tensor(code[:, :], code[:, :], digit[:, :].bitcast(F32), ALU.mult).then_inc(ev("code"), 1)
            dve.wait_ge(ev("node_iota"), 1)
            iota_c = node_iota[:, :].unsqueeze(1).to_broadcast([P, EC, N])
            V.tensor_tensor(src_hot, iota_c, spread(esrc, N), ALU.is_equal).then_inc(ev("src_hot"), 1)
            V.tensor_tensor(dst_val[:, :, :], iota_c, spread(edst, N), ALU.is_equal).then_inc(ev("dst_hot"), 1)

            dve.wait_ge(ev("upper"), 1)
            dve.wait_ge(ev("keyc"), 1)

            def duplicates(r):
                for b in range(2):
                    dve.wait_ge(ev("keys_ps"), 2 * r + b + 1)
                    for i in range(4):
                        c = 8 * r + 4 * b + i
                        if c:
                            dve.wait_ge(ev("dup"), c)
                        V.scalar_tensor_tensor(junk[:, :], bank[6 + b][:, i * P:(i + 1) * P], keyc[:, c:c + 1],
                                               upper[:, :], ALU.is_equal, ALU.mult, accum_out=dup[:, c:c + 1])\
                            .then_inc(ev("dup"), 1)

            duplicates(0)
            duplicates(1)
            dve.wait_ge(ev("etw_ln"), 1)
            V.scalar_tensor_tensor(wmask[:, :], etw_sb[:, :], 0.0, sp_a[:, :], ALU.max, ALU.add).then_inc(ev("wmask"), 1)
            features(mkT, negT, expT, "mkT", "mk")
            duplicates(2)
            dve.wait_ge(ev("dup"), EC)
            V.scalar_tensor_tensor(code[:, :], dup[:, :], 0.0, code[:, :], ALU.is_equal, ALU.mult).then_inc(ev("code"), 1)
            dve.wait_ge(ev("code"), 3)
            dve.wait_ge(ev("dst_hot"), 1)
            V.tensor_tensor(dst_val[:, :, :], dst_val[:, :, :], spread(code[:, :], N), ALU.mult).then_inc(ev("dst_val"), 1)

            def scale_rhs(c):
                st = rhs_stage[:, c % 2, :].rearrange("p (k n) -> p k n", k=KT)
                dve.wait_ge(ev("rhs_amax"), c + 1)
                sc = rscale[:, c * 256:(c + 1) * 256]
                V.tensor_scalar(sc, ramax[:, c % 2, :], ABSMAX_FLOOR, 1.0 / INT8_MAX, ALU.max, ALU.mult)\
                    .then_inc(ev("rhs_scale"), 1)
                dve.wait_ge(ev("rhs_scale"), c + 1)
                V.reciprocal(rinv[:, c % 2, :], sc).then_inc(ev("rhs_inv"), 1)
                dve.wait_ge(ev("rhs_inv"), c + 1)
                V.tensor_tensor(st, st, rinv[:, c % 2, :].unsqueeze(1).to_broadcast([P, KT, 256]), ALU.mult)\
                    .then_inc(ev("rhs_div"), 1)
                dve.wait_ge(ev("rhs_div"), c + 1)
                V.tensor_scalar(st, st, INT8_MAX, -INT8_MAX, ALU.min, ALU.max).then_inc(ev("rhs_scaled"), 1)

            def max_rhs(c):
                dve.wait_ge(ev(f"rhs_full{c % 2}"), 16 * (c // 2 + 1))
                V.tensor_reduce(ramax[:, c % 2, :], rhs_stage[:, c % 2, :].rearrange("p (k n) -> p n k", k=KT),
                                AX.X, ALU.max, apply_absolute_value=True).then_inc(ev("rhs_pmax"), 1)

            max_rhs(0)
            max_rhs(1)
            features(mqT, negT, expT, "mqT", "mq")
            for h in range(2):
                dve.wait_ge(ev("kv_ps"), h + 1)
                V.tensor_tensor(kvz[:, 0, TPB * h:TPB * (h + 1), :], bank[4 + h][:, :].rearrange("p (j n) -> p j n", j=TPB),
                                blockm[:, :].unsqueeze(1).to_broadcast([P, TPB, P]), ALU.mult).then_inc(ev("kv"), 1)
            dve.wait_ge(ev("z_ps"), 1)
            V.tensor_copy(z_sb[:, :], bank[6][:, 0:KT]).then_inc(ev("z_sb"), 1)
            dve.wait_ge(ev("z_sb"), 1)
            V.tensor_tensor(kvz[:, 1, :, :], blockm[:, :].unsqueeze(1).to_broadcast([P, KT, P]),
                            spread(z_sb[:, :], P), ALU.mult).then_inc(ev("kv"), 1)
            scale_rhs(0)
            for h in range(2):
                js = slice(TPB * h, TPB * (h + 1))
                dve.wait_ge(ev("den_ps"), h + 1)
                V.tensor_scalar(negT[:, js, :], tiles(6 + h), ATTN_EPS, None, ALU.max).then_inc(ev("den"), 1)
            dve.wait_ge(ev("den"), 2)
            V.reciprocal(negT[:, :, :], negT[:, :, :]).then_inc(ev("rden"), 1)
            dve.wait_ge(ev("rden"), 1)
            for h in range(2):
                js = slice(TPB * h, TPB * (h + 1))
                V.tensor_tensor(yT[:, js, :], tiles(4 + h), negT[:, js, :], ALU.mult).then_inc(ev("yT"), 1)
            scale_rhs(1)
            max_rhs(2)

            dve.wait_ge(ev("edge_ps"), 1)
            V.tensor_copy(esum[:, :], bank[6][0:N, 0:N]).then_inc(ev("esum"), 1)
            dve.wait_ge(ev("ident"), 1)
            V.tensor_scalar(ediag[:, :], ident[0:N, 0:N], 4.0, None, ALU.mult).then_inc(ev("ediag"), 1)
            V.tensor_scalar(far[:, :], ident[0:N, 0:N], FAR, -FAR, ALU.mult, ALU.add).then_inc(ev("far"), 1)
            dve.wait_ge(ev("esum"), 1)
            V.tensor_scalar(ecode[:, :], esum[:, :].bitcast(I32), 22, 7, ALU.logical_shift_right, ALU.bitwise_and)\
                .then_inc(ev("ecode"), 1)
            V.tensor_scalar(absent[:, :], esum[:, :], 0.0, None, ALU.is_equal).then_inc(ev("absent"), 1)
            dve.wait_ge(ev("absent"), 1)
            dve.wait_ge(ev("far"), 1)
            V.tensor_tensor(mtmp[:, :], absent[:, :], ediag[:, :], ALU.mult).then_inc(ev("mtmp"), 1)
            V.tensor_tensor(absent[:, :], absent[:, :], far[:, :], ALU.mult).then_inc(ev("absent"), 1)
            dve.wait_ge(ev("mtmp"), 1)
            dve.wait_ge(ev("ecode"), 1)
            V.tensor_tensor(ecodef[:, :], ecode[:, :], mtmp[:, :], ALU.add).then_inc(ev("ecodef"), 1)
            dve.wait_ge(ev("ecodef"), 1)
            dve.wait_ge(ev("wmask"), 1)
            prev = absent
            for i, c in enumerate((0, 2, 3, 4)):
                if i:
                    dve.wait_ge(ev("mask"), i)
                V.tensor_scalar(mtmp[:, :], ecodef[:, :], float(c), wmask[:, i:i + 1], ALU.is_equal, ALU.mult)\
                    .then_inc(ev("mtmp"), 1)
                dve.wait_ge(ev("mtmp"), 2 + i)
                dve.wait_ge(ev("absent"), 2)
                V.tensor_tensor(mask[:, :], prev[:, :], mtmp[:, :], ALU.add).then_inc(ev("mask"), 1)
                prev = mask

            for h in range(2):
                js = slice(TPB * h, TPB * (h + 1))
                dve.wait_ge(ev("owT"), h + 1)
                V.tensor_tensor(y1T[:, js, :], xnT[:, js, :], owT[:, js, :], ALU.add).then_inc(ev("y1T"), 1)
            layer_norm(2, y1_rows[:, :], ln2_rows[:, :], ("y1_rows", 1, 2))
            scale_rhs(2)
            max_rhs(3)
            affine_T((4, 5), ln2T, "g2", "be2", "ln2_tr", "ln2T")
            scale_rhs(3)

            dve.wait_ge(ev("mask"), 4)
            for g in range(4):
                hs = group_heads(g)
                pg = probs[:, hs[0]:hs[-1] + 1:2, :]
                mx = smax[:, 4 * g:4 * g + 4]
                dve.wait_ge(ev("scores_ps"), g + 1)
                V.scalar_tensor_tensor(pg, tiles([0, 1, 6, 7][g])[0:N, :, :], float(HD) ** -0.5,
                                       mask[:, :].unsqueeze(1).to_broadcast([N, 4, N]), ALU.mult, ALU.add)\
                    .then_inc(ev("scores"), 1)
                dve.wait_ge(ev("scores"), g + 1)
                V.tensor_reduce(mx, pg, AX.X, ALU.max).then_inc(ev("smax"), 1)
                dve.wait_ge(ev("smax"), g + 1)
                V.tensor_tensor(pg, pg, spread(mx, N), ALU.subtract).then_inc(ev("scores_shifted"), 1)
            for g in range(4):
                hs = group_heads(g)
                pg = probs[:, hs[0]:hs[-1] + 1:2, :]
                sm = ssum[:, 4 * g:4 * g + 4]
                rs = rsum[:, 4 * g:4 * g + 4]
                dve.wait_ge(ev("probs_exp"), g + 1)
                V.tensor_reduce(sm, pg, AX.X, ALU.add).then_inc(ev("ssum"), 1)
                dve.wait_ge(ev("ssum"), g + 1)
                V.reciprocal(rs, sm).then_inc(ev("rsum"), 1)
                dve.wait_ge(ev("rsum"), g + 1)
                V.tensor_tensor(pg, pg, spread(rs, N), ALU.mult).then_inc(ev("probs"), 1)
            for g in range(4):
                hs = group_heads(g)
                dve.wait_ge(ev("probs_tr"), g + 1)
                V.tensor_copy(probsT[:, hs[0]:hs[-1] + 1:2, :], tiles([0, 1, 6, 7][g])[0:N, :, :])\
                    .then_inc(ev("probsT"), 1)
            dve.wait_ge(ev("base"), 1)
            dve.wait_ge(ev("chunk_done"), CHUNKS)
            for h in range(2):
                cs = slice(h * HALF, (h + 1) * HALF)
                V.tensor_tensor(x1_rows[:, cs], bank[4 + h][0:N, :], base_rows[:, cs], ALU.add).then_inc(ev("x1"), 1)
            layer_norm(3, x1_rows[:, :], xl_rows[:, :], ("x1", 1, 2))
            dve.wait_ge(ev("ln_done"), 4)
            amax, ls, linv = (lscale[:, i:i + 1] for i in range(3))
            V.tensor_reduce(amax, xl_rows[:, :], AX.X, ALU.max, apply_absolute_value=True).then_inc(ev("lq"), 1)
            dve.wait_ge(ev("lq"), 1)
            V.tensor_scalar(ls, amax, ABSMAX_FLOOR, 1.0 / INT8_MAX, ALU.max, ALU.mult).then_inc(ev("lq"), 1)
            dve.wait_ge(ev("lq"), 2)
            V.reciprocal(linv, ls).then_inc(ev("lq"), 1)
            dve.wait_ge(ev("lq"), 3)
            for h in range(2):
                cs = slice(h * HALF, (h + 1) * HALF)
                V.tensor_scalar(xl_rows[:, cs], xl_rows[:, cs], linv, INT8_MAX, ALU.mult, ALU.min).then_inc(ev("lq"), 1)
            for h in range(2):
                cs = slice(h * HALF, (h + 1) * HALF)
                dve.wait_ge(ev("lq"), 4 + h)
                V.tensor_scalar(xl_rows[:, cs], xl_rows[:, cs], -INT8_MAX, ROUND, ALU.max, ALU.add).then_inc(ev("lq"), 1)
            for h in range(2):
                cs = slice(h * HALF, (h + 1) * HALF)
                dve.wait_ge(ev("lq"), 6 + h)
                V.tensor_scalar(q_rows[:, cs], xl_rows[:, cs], ROUND, None, ALU.subtract).then_inc(ev("q_rows"), 1)
            for h in range(2):
                js = slice(TPB * h, TPB * (h + 1))
                dve.wait_ge(ev("q8_tr"), h + 1)
                V.tensor_copy(q8T[:, js, :], bank[h][:, 0:TPB * N // 2].bitcast(BF16)
                              .rearrange("p (j n) -> p j n", j=TPB)).then_inc(ev("q8T"), 1)
            for h in range(2):
                cs = slice(h * HALF, (h + 1) * HALF)
                dve.wait_ge(ev("ffn_ps"), h + 1)
                V.scalar_tensor_tensor(xl_rows[:, cs], bank[6 + h][0:N, :], ls, rscale[0:N, cs], ALU.mult, ALU.mult)\
                    .then_inc(ev("ffn"), 1)
                dve.wait_ge(ev("ffn"), h + 1)
                V.tensor_tensor(x1_rows[:, cs], x1_rows[:, cs], xl_rows[:, cs], ALU.add).then_inc(ev("out_ready"), 1)

        @block.tensor
        def _(pe):
            T = nc.tensor

            def chunk_arrived(w, q):
                c = FIRST[w] + q
                pe.wait_ge(ev(f"slot_full{c % RING}"), 16 * (c // RING + 1))

            def project_T(w, src, banks, src_ready, banks_free=()):
                for name, value in (*src_ready, *banks_free):
                    pe.wait_ge(ev(name), value)
                for q in range(4):
                    chunk_arrived(w, q)
                    for j in (2 * q, 2 * q + 1):
                        for k in range(KT):
                            ins = T.matmul(tiles(banks[j // TPB])[:, j % TPB, :],
                                           slot(w, q)[:, ((j % 2) * KT + k) * P:((j % 2) * KT + k + 1) * P],
                                           src[:, k, :], start=(k == 0), stop=(k == KT - 1))
                    ins.then_inc(ev("chunk_done"), 1)

            def rows_to_T(src, banks, src_ready, name):
                for n, v in src_ready:
                    pe.wait_ge(ev(n), v)
                for h in range(2):
                    for j in range(TPB * h, TPB * h + TPB):
                        ins = T.transpose(tiles(banks[h])[:, j % TPB, :], src[:, j * P:(j + 1) * P], ident[0:N, 0:N])
                    ins.then_inc(ev(name), 1)

            def T_to_rows(src, banks, src_ready, name):
                for h in range(2):
                    for n, v in src_ready:
                        pe.wait_ge(ev(n), v if n not in ("y1T", "v2T", "mvT") else h + 1)
                    for j in range(TPB * h, TPB * h + TPB):
                        ins = T.transpose(bank[banks[h]][0:N, (j % TPB) * P:(j % TPB + 1) * P], src[:, j, :], ident[:, :])
                    ins.then_inc(ev(name), 1)

            def keys(r):
                if r == 0:
                    pe.wait_ge(ev("keyrow"), 1)
                    pe.wait_ge(ev("keyw"), 1)
                    pe.wait_ge(ev("rowbias_out"), 2)
                else:
                    pe.wait_ge(ev("dup"), 8 * r)
                for b in range(2):
                    o = (2 * r + b) * HALF
                    T.matmul(bank[6 + b][:, :], keyw[:, :], keyrow[:, o:o + HALF], start=True, stop=True)\
                        .then_inc(ev("keys_ps"), 1)

            pe.wait_ge(ev("rowb_loaded"), 16)
            pe.wait_ge(ev("ones"), 1)
            for h in range(2):
                T.matmul(bank[6 + h][0:N, :], ones[0:2, 0:N], rowb[:, h * HALF:(h + 1) * HALF], start=True, stop=True)\
                    .then_inc(ev("rowbias_ps"), 1)
            rows_to_T(xn_rows, (0, 1), (("ident", 1), ("ln_done", 1)), "xn_tr")
            project_T("q", xnT, (2, 3), (("xnT", 2),))
            rows_to_T(ln_rows, (4, 5), (("ln_done", 2),), "lnx_tr")
            keys(0)
            project_T("mk", lnT, (0, 1), (("lnT", 2),))
            keys(1)
            project_T("mv", lnT, (2, 3), (("qT", 2),))
            keys(2)
            project_T("k", xnT, (0, 1), (("mkT", 2),))
            T_to_rows(mkT, (4, 5), (("mk_feat", 1), ("lnT", 2)), "kf_tr")
            T_to_rows(mvT, (6, 7), (("mvT", 2), ("dup", EC)), "mv_tr")
            project_T("mq", lnT, (2, 3), (("mvT", 2),))
            pe.wait_ge(ev("kf_rows"), 2)
            pe.wait_ge(ev("mv_rows"), 2)
            for j in range(KT):
                js = slice(j * P, (j + 1) * P)
                ins = T.matmul(bank[4 + j // TPB][:, (j % TPB) * P:(j % TPB + 1) * P], kf_rows[:, js], mv_rows[:, js],
                               start=True, stop=True)
                if j % TPB == TPB - 1:
                    ins.then_inc(ev("kv_ps"), 1)
            for j in range(KT):
                ins = T.matmul(bank[6][:, j:j + 1], kf_rows[:, j * P:(j + 1) * P], ones[0:N, 0:1], start=True, stop=True)
            ins.then_inc(ev("z_ps"), 1)
            project_T("v", xnT, (0, 1), (("kT", 2),))
            pe.wait_ge(ev("kv"), 3)
            pe.wait_ge(ev("mq_feat"), 1)
            for what in range(2):
                for j in range(KT):
                    ins = T.matmul(tiles(4 + 2 * what + j // TPB)[:, j % TPB, :], kvz[:, what, j, :], mqT[:, j, :],
                                   start=True, stop=True)
                    if what == 1 and j % TPB == TPB - 1:
                        ins.then_inc(ev("den_ps"), 1)
                if what == 0:
                    ins.then_inc(ev("num_ps"), 1)
            project_T("q2", qT, (2, 3), (("mqT", 2),))
            pe.wait_ge(ev("den"), 2)
            pe.wait_ge(ev("src_hot"), 1)
            pe.wait_ge(ev("dst_val"), 1)
            for c in range(EC):
                ins = T.matmul(bank[6][0:N, 0:N], src_hot[:, c, :], dst_val[:, c, :], start=(c == 0), stop=(c == EC - 1))
            ins.then_inc(ev("edge_ps"), 1)
            project_T("ow", yT, (0, 1), (("yT", 2), ("vT", 2)))
            project_T("k2", kT, (2, 3), (("q2T", 2),))
            T_to_rows(y1T, (4, 5), (("y1T", 2), ("ident", 1)), "y1_tr")
            pe.wait_ge(ev("k2T"), 2)
            pe.wait_ge(ev("owT"), 2)
            pe.wait_ge(ev("esum"), 1)
            for g in range(4):
                for i, h in enumerate(group_heads(g)):
                    r = slice(HD * (h % 2), HD * (h % 2) + HD)
                    ins = T.matmul(tiles([0, 1, 6, 7][g])[0:N, i, :], q2T[r, h // 2, :], k2T[r, h // 2, :],
                                   start=True, stop=True)
                ins.then_inc(ev("scores_ps"), 1)
            rows_to_T(ln2_rows, (4, 5), (("ln_done", 3),), "ln2_tr")
            pe.wait_ge(ev("ln2T"), 2)
            chunk_arrived("w12", 0)
            w1 = slot("w12", 0)[:, 0:D]
            w2 = slot("w12", 0)[:, D:2 * D]
            for k in range(KT):
                ins = T.matmul(bank[4][:, 0:N], w1[:, k * P:(k + 1) * P], ln2T[:, k, :], start=(k == 0), stop=(k == KT - 1))
            ins.then_inc(ev("h_ps"), 1)
            pe.wait_ge(ev("hT"), 1)
            for h in range(2):
                ins = T.matmul(bank[4 + h][0:N, :], hT[:, :], w2[:, h * HALF:(h + 1) * HALF], start=True, stop=False,
                               skip_group_check=True)
            ins.then_inc(ev("chunk_done"), 1)
            project_T("v2", vT, (2, 3), (("k2T", 2),))
            for g in range(4):
                pe.wait_ge(ev("probs"), g + 1)
                for i, h in enumerate(group_heads(g)):
                    ins = T.transpose(tiles([0, 1, 6, 7][g])[0:N, i, :], probs[:, h, :], ident[0:N, 0:N])
                ins.then_inc(ev("probs_tr"), 1)
            T_to_rows(v2T, (0, 1), (("v2T", 2), ("probsT", 2)), "v2_tr")
            pe.wait_ge(ev("v2_rows"), 2)
            pe.wait_ge(ev("probsT"), 4)
            for h in range(H):
                r = slice(HD * (h % 2), HD * (h % 2) + HD)
                ins = T.matmul(tiles(2 + h // 8)[r, (h % 8) // 2, :], v2_rows[:, h * HD:(h + 1) * HD], probsT[:, h, :],
                               start=True, stop=True)
                if h % 8 == 7:
                    ins.then_inc(ev("pv_ps"), 1)
            for q in range(4):
                chunk_arrived("wo", q)
                pe.wait_ge(ev("aT"), 1 + q // 2)
                for k in (2 * q, 2 * q + 1):
                    for h in range(2):
                        ins = T.matmul(bank[4 + h][0:N, :], aT[:, k, :],
                                       slot("wo", q)[:, (k % 2) * D + h * HALF:(k % 2) * D + (h + 1) * HALF],
                                       start=False, stop=(k == KT - 1), skip_group_check=True)
                ins.then_inc(ev("chunk_done"), 1)
            pe.wait_ge(ev("identb"), 1)
            for h in range(2):
                pe.wait_ge(ev("q_rows"), h + 1)
                for j in range(TPB * h, TPB * h + TPB):
                    ins = T.transpose(bank[h][:, 0:TPB * N // 2].bitcast(BF16)[:, (j % TPB) * N:(j % TPB + 1) * N],
                                      q_rows[:, j * P:(j + 1) * P], identb[0:N, 0:N])
                ins.then_inc(ev("q8_tr"), 1)
            pe.wait_ge(ev("q8T"), 2)
            pe.wait_ge(ev("rhs_rounded"), 4)
            for c in range(4):
                for k in range(KT):
                    ins = T.matmul(bank[6 + c // 2][0:N, (c % 2) * 256:(c % 2) * 256 + 256], q8T[:, k, :],
                                   rhs_q[:, c, k * 256:(k + 1) * 256], start=(k == 0), stop=(k == KT - 1))
                if c % 2:
                    ins.then_inc(ev("ffn_ps"), 1)


def kernel(**inputs):
    import numpy as np
    from concourse import bacc
    from concourse.bass_utils import run_bass_kernel_spmd

    a = {k: np.ascontiguousarray(v) for k, v in inputs.items()}
    g, m = "L0_gnn_", "L0_mix_"

    def blocks_T(w):
        return w.reshape(KT, P, 4, 2, P).transpose(2, 1, 3, 0, 4).reshape(4, P, CHUNK)

    def blocks_rows(w):
        return w.reshape(4, 2, P, D).transpose(0, 2, 1, 3).reshape(4, P, CHUNK)

    qkv = a[m + "qkv_w"]
    parts = {
        "q": blocks_T(a[g + "wq"].T), "k": blocks_T(a[g + "wk"].T), "v": blocks_T(a[g + "wv"].T),
        "q2": blocks_T(a[g + "wiq"].T), "k2": blocks_T(a[g + "wik"].T), "v2": blocks_T(a[g + "wiv"].T),
        "mq": blocks_T(qkv[:, 0:D]), "mk": blocks_T(qkv[:, D:2 * D]), "mv": blocks_T(qkv[:, 2 * D:3 * D]),
        "ow": blocks_T(a[m + "out_w"]), "wo": blocks_rows(a[g + "wo"].T),
        "w12": np.concatenate([a[m + "w1"].reshape(KT, P, P).transpose(1, 0, 2).reshape(P, D), a[m + "w2"]], axis=1)[None],
    }
    weights = np.ascontiguousarray(np.concatenate([parts[w] for w in ORDER]))
    vectors = {
        "bq": a[g + "bq"], "bk": a[g + "bk"], "bv": a[g + "bv"], "biq": a[g + "biq"], "bik": a[g + "bik"],
        "biv": a[g + "biv"], "mqb": a[m + "qkv_b"][0:D], "mkb": a[m + "qkv_b"][D:2 * D], "mvb": a[m + "qkv_b"][2 * D:],
        "outb": a[m + "out_b"], "g1": a[m + "g1"], "be1": a[m + "be1"], "g2": a[m + "g2"], "be2": a[m + "be2"],
    }
    arrays = {
        "x_in": a["x"],
        "weights": weights,
        "rhs": np.ascontiguousarray(a["L0_ffn_rhs"].reshape(KT, P, 4, 256).transpose(2, 1, 0, 3).reshape(4, P, CHUNK)),
        "cols": np.ascontiguousarray(np.concatenate([vectors[n].reshape(KT, P).T for n in COLS] + [a[m + "b1"][:, None]], axis=1)),
        "rowbias": np.ascontiguousarray(np.stack([a[g + "bo"], a[m + "b2"]])),
        "edge_cols": np.ascontiguousarray(np.stack([a[n].reshape(EC, P).T for n in ("src", "dst", "edge_type_5")], axis=1)),
        "edge_rows": np.ascontiguousarray(np.stack([a["src"], a["dst"]])),
        "etw": np.ascontiguousarray(np.broadcast_to(a[g + "edge_type_weights"], (N, 4))),
    }
    nc = bacc.Bacc("TRN2", target_bir_lowering=False, num_devices=1)
    aps = [nc.dram_tensor(n, v.shape, mybir.dt.from_np(v.dtype), kind="ExternalInput").ap() for n, v in arrays.items()]
    out = nc.dram_tensor("out_rows", (N, D), F32, kind="ExternalOutput").ap()
    build(nc, *aps, out)
    r = run_bass_kernel_spmd(nc, [arrays], core_ids=[0])
    return r.results[0]["out_rows"]
```

```python
from contextlib import ExitStack

import concourse.bass as bass
from concourse import mybir

F32 = mybir.dt.float32
BF16 = mybir.dt.bfloat16
I32 = mybir.dt.int32
ALU = mybir.AluOpType
ACT = mybir.ActivationFunctionType
AX = mybir.AxisListType

P = 128
N = 96
D = 1024
KT = D // P
H = 16
HD = D // H
E = 3072
EC = E // P
HALF = 512
QUARTER = 256
PIECES = ((2, 0, HALF), (3, HALF, QUARTER), (0, HALF + QUARTER, QUARTER))
FFN_BANKS = (6, 7, 2, 3)
TPB = KT // 2
LN_EPS = 1e-5
ATTN_EPS = 1e-6
ABSMAX_FLOOR = 1e-12
INT8_MAX = 127.0
ROUND = 1.5 * 2.0 ** 23
FAR = 1e30
DIGIT = 4
DIGIT0 = 80

ORDER = ["q", "mk", "mv", "mq", "k", "v", "q2", "ow", "k2", "v2", "w12", "wo"]
CHUNK = 2 * D
RING = 9
HEAD_WARM = 12
TAIL_WARM = 20
RHS_AFTER = 6
FIRST = {}
_n = 0
for _w in ORDER:
    FIRST[_w] = _n
    _n += 1 if _w == "w12" else 4
CHUNKS = _n

COLS = ["bq", "bk", "bv", "biq", "bik", "biv", "mqb", "mkb", "mvb", "outb", "g1", "be1", "g2", "be2"]
COL = {name: KT * i for i, name in enumerate(COLS)}
COL_B1 = KT * len(COLS)
NCOLS = COL_B1 + 1


def build(nc, x, weights, rhs, cols, rowbias, edge_cols, edge_rows, etw, out):
    assert CHUNKS % RING == 0
    with ExitStack() as ctx:
        sems = {}

        def ev(name):
            if name not in sems:
                sems[name] = ctx.enter_context(nc.semaphore(name))
            return sems[name]

        def sb(name, shape, dt=F32):
            return ctx.enter_context(nc.sbuf_tensor(name, shape, dt))

        ring = sb("ring", [P, RING, CHUNK])
        rhs_stage = sb("rhs_stage", [P, 2, CHUNK])
        rhs_q = sb("rhs_q", [P, 4, CHUNK], BF16)
        x_rows = sb("x_rows", [N, D])
        xn_rows = sb("xn_rows", [N, D])
        ln_rows = sb("ln_rows", [N, D])
        base_rows = sb("base_rows", [N, D])
        xnT = sb("xnT", [P, KT, N])
        lnT = sb("lnT", [P, KT, N])
        qT = sb("qT", [P, KT, N])
        kT = sb("kT", [P, KT, N])
        vT = sb("vT", [P, KT, N])
        mqT = sb("mqT", [P, KT, N])
        mkT = sb("mkT", [P, KT, N])
        mvT = sb("mvT", [P, KT, N])
        negT = sb("negT", [P, KT, N])
        expT = sb("expT", [P, KT, N])
        kf_rows = sb("kf_rows", [N, D])
        mv_rows = sb("mv_rows", [N, D])
        kvz = sb("kvz", [P, 2, KT, P])
        yT = sb("yT", [P, KT, N])
        late = sb("late", [P, E // 2 + EC * N // 2])
        cols_sb = sb("cols_sb", [P, NCOLS])
        rowb = sb("rowb", [2, D])
        hT = sb("hT", [P, N])
        ident = sb("ident", [P, P])
        identb = sb("identb", [P, P], BF16)
        upper = sb("upper", [P, P])
        blockm = sb("blockm", [P, P])
        ones = sb("ones", [P, P])
        keyw = sb("keyw", [2, P], BF16)
        node_iota = sb("node_iota", [P, N])
        digit_exp = sb("digit_exp", [P, EC], I32)
        digit = sb("digit", [P, EC], I32)
        edge_i = sb("edge_i", [P, 3, EC], I32)
        edge_f = sb("edge_f", [P, 3, EC])
        keyc = sb("keyc", [P, EC])
        dup = sb("dup", [P, EC])
        code = sb("code", [P, EC])
        is0 = sb("is0", [P, EC])
        junk = sb("junk", [P, P])
        dst_val = sb("dst_val", [P, EC, N], BF16)
        etw_sb = sb("etw_sb", [N, 4])
        sp_a = sb("sp_a", [N, 4])
        sp_b = sb("sp_b", [N, 4])
        wmask = sb("wmask", [N, 4])
        ediag = sb("ediag", [N, N])
        far = sb("far", [N, N])
        esum = sb("esum", [N, N])
        ecode = sb("ecode", [N, N], I32)
        ecodef = sb("ecodef", [N, N])
        absent = sb("absent", [N, N])
        mask = sb("mask", [N, N])
        mtmp = sb("mtmp", [N, N])
        z_sb = sb("z_sb", [P, KT])
        stats = sb("stats", [N, 3, 2, 6])
        stats_x1 = sb("stats_x1", [N, 4, 6])
        mv = sb("mv", [N, 4, 2])
        extremes = sb("extremes", [N, 2, 3])
        sd = sb("sd", [N, 4])
        rstd = sb("rstd", [N, 4])
        smax = sb("smax", [N, H])
        ssum = sb("ssum", [N, H])
        rsum = sb("rsum", [N, H])
        lscale = sb("lscale", [N, 4])
        ramax = sb("ramax", [P, 2, 256])
        rinv = sb("rinv", [P, 2, 256])
        rscale = sb("rscale", [P, D])
        q8T = sb("q8T", [P, KT, N], BF16)
        eps = sb("eps", [N, 1])
        warm = sb("warm", [N, 3])

        y1T, owT = xnT, expT
        q2T, k2T, aT = mqT, mkT, vT
        y1_rows = kf_rows
        ln2_rows, ln2T = mv_rows, lnT
        probs = kvz[:, :, :, :].rearrange("p a b c -> p (a b c)")[0:N, 0:H * N].rearrange("p (h n) -> p h n", h=H)
        x1_rows, xl_rows = xn_rows, ln_rows
        q_rows = mv_rows[:, 0:D // 2].bitcast(BF16)
        probsT = late[0:N, 0:H * N].rearrange("p (h n) -> p h n", h=H)
        v2_rows = late[0:N, H * N:H * N + D]
        keyrow = late[0:2, 0:E // 2].bitcast(BF16)
        src_hot = late[:, E // 2:E // 2 + EC * N // 2].bitcast(BF16).rearrange("p (c n) -> p c n", c=EC)
        edge_row_i = rhs_q[:, :, :].rearrange("p a b -> p (a b)")[0:2, 0:2 * E].bitcast(I32)

        bank = [ctx.enter_context(nc.psum_tensor(f"bank{i}", [P, HALF], F32)) for i in range(8)]

        def slot(w, q):
            return ring[:, (FIRST[w] + q) % RING, :]

        def chunk_count(w, q):
            return FIRST[w] + q + 1

        def tiles(b):
            return bank[b][:, 0:TPB * N].rearrange("p (j n) -> p j n", j=TPB)

        def col(name, j0, j1):
            return cols_sb[:, COL[name] + j0:COL[name] + j1]

        def spread(ap, n):
            return ap.unsqueeze(2).to_broadcast([ap.shape[0], ap.shape[1], n])

        def group_heads(g):
            return range(8 * (g // 2) + g % 2, 8 * (g // 2) + 8, 2)

        block = ctx.enter_context(nc.Block())

        @block.sync
        def _(sp):
            sp.dma_start(x_rows[:, :], x).then_inc(ev("x_loaded"), 16)
            sp.dma_start(cols_sb[:, :], cols).then_inc(ev("cols_loaded"), 16)
            sp.dma_start(rowb[:, :], rowbias).then_inc(ev("rowb_loaded"), 16)
            sp.dma_start(etw_sb[:, :], etw).then_inc(ev("etw_loaded"), 16)
            for s in range(RING):
                sp.dma_start(ring[:, s, :], weights[s]).then_inc(ev(f"slot_full{s}"), 16)
            with sp.Fori(1, CHUNKS // RING) as r:
                for s in range(RING):
                    sp.wait_ge(ev("chunk_done"), r * RING + (s + 1 - RING))
                    sp.dma_start(ring[:, s, :], weights[bass.ds(r * RING + s, 1)].rearrange("a p n -> (a p) n"))\
                        .then_inc(ev(f"slot_full{s}"), 16)
            for c in range(4):
                cs = slice(c * QUARTER, (c + 1) * QUARTER)
                if c < 2:
                    sp.wait_ge(ev("out_ready_pool"), c + 1)
                else:
                    sp.wait_ge(ev("out_ready"), c - 1)
                sp.dma_start(out[:, cs], x1_rows[:, cs]).then_inc(ev("out_stored"), 16)
            sp.wait_ge(ev("out_stored"), 64)

        @block.gpsimd
        def _(pool):
            pool.memset(ident[:, :], 0.0).then_inc(ev("zeros"), 1)
            pool.memset(identb[:, :], 0.0).then_inc(ev("zeros"), 1)
            pool.memset(upper[:, :], 1.0).then_inc(ev("zeros"), 1)
            pool.wait_ge(ev("zeros"), 3)
            pool.affine_select(out=ident[:, :], in_=ident[:, :], compare_op=ALU.not_equal, fill=1.0, base=0,
                               pattern=[[-1, P]], channel_multiplier=1).then_inc(ev("ident"), 1)
            pool.affine_select(out=identb[:, :], in_=identb[:, :], compare_op=ALU.not_equal, fill=1.0, base=0,
                               pattern=[[-1, P]], channel_multiplier=1).then_inc(ev("identb"), 1)
            pool.affine_select(out=upper[:, :], in_=upper[:, :], compare_op=ALU.is_ge, fill=0.0, base=-1,
                               pattern=[[1, P]], channel_multiplier=-1).then_inc(ev("upper"), 1)
            pool.iota(node_iota[:, :], [[1, N]], base=0, channel_multiplier=0,
                      allow_small_or_imprecise_dtypes=True).then_inc(ev("node_iota"), 1)
            pool.iota(digit_exp[:, :], [[DIGIT, EC]], base=DIGIT0, channel_multiplier=0).then_inc(ev("digit_exp"), 1)
            pool.wait_ge(ev("edge_cols_loaded"), 16)
            pool.tensor_copy(edge_f[:, :, :], edge_i[:, :, :]).then_inc(ev("edge_f"), 1)

            pool.wait_ge(ev("x_loaded"), 16)
            pool.wait_ge(ev("rowbias_out"), 2)
            pool.tensor_tensor(base_rows[:, :], x_rows[:, :], base_rows[:, :], ALU.add).then_inc(ev("base0"), 1)

            pool.wait_ge(ev("chunk_done"), RHS_AFTER)
            for c in range(2):
                pool.dma_start(rhs_stage[:, c, :], rhs[c]).then_inc(ev(f"rhs_full{c}"), 16)
            for c in range(4):
                pool.wait_ge(ev("rhs_pmax"), c + 1)
                pool.partition_all_reduce(ramax[:, c % 2, :], ramax[:, c % 2, :], P,
                                          bass.bass_isa.ReduceOp.max).then_inc(ev("rhs_amax"), 1)
                if c + 2 < 4:
                    pool.wait_ge(ev("rhs_rounded"), c + 1)
                    pool.dma_start(rhs_stage[:, c % 2, :], rhs[c + 2]).then_inc(ev(f"rhs_full{c % 2}"), 16)
            pool.wait_ge(ev("base0"), 1)
            pool.wait_ge(ev("y1_rows"), 2)
            pool.tensor_tensor(base_rows[:, :], base_rows[:, :], y1_rows[:, :], ALU.add).then_inc(ev("base"), 1)
            for c in range(2):
                cs = slice(c * QUARTER, (c + 1) * QUARTER)
                pool.wait_ge(ev("ffn"), c + 1)
                pool.tensor_tensor(x1_rows[:, cs], x1_rows[:, cs], xl_rows[:, cs], ALU.add).then_inc(ev("out_ready_pool"), 1)

        @block.scalar
        def _(act):
            A = nc.scalar
            act.wait_ge(ev("eps_set"), 1)
            A.activation(warm[:, 0:1], eps[:, :], ACT.Sqrt).then_inc(ev("warm"), 1)
            act.dma_start(edge_i[:, :, :], edge_cols).then_inc(ev("edge_cols_loaded"), 16)
            act.dma_start(edge_row_i, edge_rows).then_inc(ev("edge_rows_loaded"), 16)

            def deviation(i):
                act.wait_ge(ev("ln_stats"), i + 1)
                A.activation(sd[:, i:i + 1], mv[:, i, 1:2], ACT.Sqrt, bias=eps[:, :]).then_inc(ev("ln_sd"), 1)

            def add_bias(banks, h, dst, bias, name):
                for j in range(TPB * h, TPB * h + TPB):
                    ins = A.activation(dst[:, j, :], tiles(banks[h])[:, j % TPB, :], ACT.Identity,
                                       bias=col(bias, j, j + 1))
                ins.then_inc(ev(name), 1)

            def drain_T(w, banks, dst, bias, name):
                for h in range(2):
                    act.wait_ge(ev("chunk_done"), chunk_count(w, 2 * h + 1))
                    add_bias(banks, h, dst, bias, name)

            def copy_rows(dst, banks, ready, name):
                for h in range(2):
                    act.wait_ge(ev(ready), h + 1)
                    A.activation(dst[:, h * HALF:(h + 1) * HALF], bank[banks[h]][0:N, :], ACT.Copy).then_inc(ev(name), 1)

            def round_rhs(c):
                act.wait_ge(ev("rhs_scaled"), c + 1)
                st = rhs_stage[:, c % 2, :]
                A.activation(st, st, ACT.Copy, bias=ROUND).then_inc(ev("rhs_magic"), 1)
                act.wait_ge(ev("rhs_magic"), c + 1)
                A.activation(rhs_q[:, c, :], st, ACT.Copy, bias=-ROUND).then_inc(ev("rhs_rounded"), 1)

            deviation(0)
            act.wait_ge(ev("xn_tr"), 1)
            A.activation(xnT[:, 0:TPB, :], tiles(0), ACT.Copy).then_inc(ev("xnT_a"), 1)
            deviation(1)
            act.wait_ge(ev("edge_rows_loaded"), 16)
            A.activation(keyrow, edge_row_i, ACT.Copy).then_inc(ev("keyrow"), 1)
            copy_rows(base_rows, (0, 1), "rowbias_ps", "rowbias_out")
            act.wait_ge(ev("etw_loaded"), 16)
            A.activation(sp_a[:, :], etw_sb[:, :], ACT.Abs).then_inc(ev("etw_abs"), 1)
            act.wait_ge(ev("etw_abs"), 1)
            A.activation(sp_b[:, :], sp_a[:, :], ACT.Exp, scale=-1.0).then_inc(ev("etw_exp"), 1)
            act.wait_ge(ev("etw_exp"), 1)
            A.activation(sp_a[:, :], sp_b[:, :], ACT.Ln, bias=1.0).then_inc(ev("etw_ln"), 1)
            act.wait_ge(ev("cols_loaded"), 16)
            drain_T("q", (2, 3), qT, "bq", "qT")
            drain_T("mk", (0, 1), mkT, "mkb", "mkT")
            act.wait_ge(ev("mk_neg"), 1)
            A.activation(expT[:, :, :], negT[:, :, :], ACT.Exp).then_inc(ev("mk_exp"), 1)
            drain_T("mv", (2, 3), mvT, "mvb", "mvT")
            copy_rows(kf_rows, (4, 5), "kf_tr", "kf_rows")
            copy_rows(mv_rows, (6, 7), "mv_tr", "mv_rows")
            drain_T("mq", (0, 1), mqT, "mqb", "mqT")
            act.wait_ge(ev("mq_neg"), 1)
            A.activation(expT[:, :, :], negT[:, :, :], ACT.Exp).then_inc(ev("mq_exp"), 1)
            round_rhs(0)
            drain_T("k", (2, 3), kT, "bk", "kT")
            round_rhs(1)
            drain_T("v", (0, 1), vT, "bv", "vT")
            round_rhs(2)
            drain_T("q2", (2, 3), q2T, "biq", "q2T")
            round_rhs(3)
            drain_T("ow", (0, 1), owT, "outb", "owT")
            copy_rows(y1_rows, (4, 5), "y1_tr", "y1_rows")
            deviation(2)
            drain_T("k2", (2, 3), k2T, "bik", "k2T")

            for g in range(4):
                act.wait_ge(ev("scores_shifted"), g + 1)
                hs = group_heads(g)
                pg = probs[:, hs[0]:hs[-1] + 1:2, :]
                A.activation(pg, pg, ACT.Exp).then_inc(ev("probs_exp"), 1)
            act.wait_ge(ev("chunk_done"), chunk_count("v2", 3))
            for h in range(2):
                A.activation(v2_rows[:, h * HALF:(h + 1) * HALF], bank[h][0:N, :], ACT.Copy).then_inc(ev("v2_rows"), 1)
            for g in (1, 3):
                hs = group_heads(g)
                act.wait_ge(ev("probs_tr"), g + 1)
                A.activation(probsT[:, hs[0]:hs[-1] + 1:2, :], tiles(4 + g)[0:N, :, :], ACT.Copy)\
                    .then_inc(ev("probsT_odd"), 1)
            for h in range(2):
                act.wait_ge(ev("pv_ps"), h + 1)
                add_bias((0, 1), h, aT, "biv", "aT")
            A.activation(warm[:, 1:2], eps[:, :], ACT.Gelu).then_inc(ev("warm"), 1)
            act.wait_ge(ev("h_ps"), 1)
            A.activation(hT[:, :], bank[6][:, 0:N], ACT.Gelu, bias=cols_sb[:, COL_B1:COL_B1 + 1]).then_inc(ev("hT"), 1)
            A.activation(warm[:, 2:3], eps[:, :], ACT.Sqrt).then_inc(ev("warm"), 1)
            deviation(3)
            act.wait_ge(ev("q8_tr"), 2)
            A.activation(q8T[:, TPB:KT, :], bank[5][:, 0:TPB * N // 2].bitcast(BF16)
                         .rearrange("p (j n) -> p j n", j=TPB), ACT.Copy).then_inc(ev("q8T_b"), 1)

        @block.vector
        def _(dve):
            V = nc.vector

            def norm_stats(i, h, src):
                V.bn_stats(stats[:, i, h, :], src[:, h * HALF:(h + 1) * HALF]).then_inc(ev("bn"), 1)

            def norm_mean(i):
                dve.wait_ge(ev("bn"), 2 * i + 2)
                V.bn_aggr(mv[:, i, :], stats[:, i, :, :]).then_inc(ev("ln_stats"), 1)

            def norm_rstd(i):
                dve.wait_ge(ev("ln_sd"), i + 1)
                V.reciprocal(rstd[:, i:i + 1], sd[:, i:i + 1]).then_inc(ev("ln_rstd"), 1)
                dve.wait_ge(ev("ln_rstd"), i + 1)

            def layer_norm(i, src, dst, ready, values):
                for h in range(2):
                    dve.wait_ge(ev(ready), values[h])
                    norm_stats(i, h, src)
                norm_mean(i)
                norm_rstd(i)
                V.tensor_scalar(dst, src, mv[:, i, 0:1], rstd[:, i:i + 1], ALU.subtract, ALU.mult)\
                    .then_inc(ev("ln_done"), 1)

            def affine_T(banks, dst, g, b, ps_ready, name):
                for h in range(2):
                    js = slice(TPB * h, TPB * (h + 1))
                    dve.wait_ge(ev(ps_ready), h + 1)
                    V.tensor_tensor(dst[:, js, :], tiles(banks[h]), spread(col(g, js.start, js.stop), N), ALU.mult)\
                        .then_inc(ev(name + "_g"), 1)
                    dve.wait_ge(ev(name + "_g"), h + 1)
                    V.tensor_tensor(dst[:, js, :], dst[:, js, :], spread(col(b, js.start, js.stop), N), ALU.add)\
                        .then_inc(ev(name), 1)

            def features(src, neg, exp, ready, name):
                dve.wait_ge(ev(ready), 2)
                V.tensor_scalar(neg[:, :, :], src[:, :, :], 0.0, None, ALU.min).then_inc(ev(name + "_neg"), 1)
                dve.wait_ge(ev(name + "_exp"), 1)
                V.scalar_tensor_tensor(src[:, :, :], src[:, :, :], 0.0, exp[:, :, :], ALU.max, ALU.add)\
                    .then_inc(ev(name + "_feat"), 1)

            V.memset(eps[:, :], LN_EPS).then_inc(ev("eps_set"), 1)
            V.memset(ones[:, :], 1.0).then_inc(ev("ones"), 1)
            V.memset(keyw[:, :], 1.0).then_inc(ev("keyw0"), 1)
            V.memset(blockm[:, :], 0.0).then_inc(ev("blockm0"), 1)
            dve.wait_ge(ev("keyw0"), 1)
            V.memset(keyw[0:1, :], float(P)).then_inc(ev("keyw"), 1)
            dve.wait_ge(ev("blockm0"), 1)
            V.memset(blockm[0:HD, 0:HD], 1.0).then_inc(ev("blockm"), 1)
            V.memset(blockm[HD:P, HD:P], 1.0).then_inc(ev("blockm"), 1)

            layer_norm(0, x_rows[:, :], xn_rows[:, :], "x_loaded", (16, 16))
            dve.wait_ge(ev("ln_done"), 1)
            norm_stats(1, 0, xn_rows)
            dve.wait_ge(ev("xn_tr"), 2)
            V.tensor_copy(xnT[:, TPB:KT, :], tiles(1)).then_inc(ev("xnT_b"), 1)
            norm_stats(1, 1, xn_rows)
            norm_mean(1)
            norm_rstd(1)
            V.tensor_scalar(ln_rows[:, :], xn_rows[:, :], mv[:, 1, 0:1], rstd[:, 1:2], ALU.subtract, ALU.mult)\
                .then_inc(ev("ln_done"), 1)

            dve.wait_ge(ev("edge_f"), 1)
            esrc, edst, etype = (edge_f[:, i, :] for i in range(3))
            V.scalar_tensor_tensor(keyc[:, :], esrc, float(P), edst, ALU.mult, ALU.add).then_inc(ev("keyc"), 1)
            V.tensor_scalar(is0[:, :], etype, 0.0, 4.0, ALU.is_equal, ALU.mult).then_inc(ev("is0"), 1)
            dve.wait_ge(ev("digit_exp"), 1)
            V.tensor_scalar(digit[:, :], digit_exp[:, :], 23, None, ALU.logical_shift_left).then_inc(ev("digit"), 1)
            dve.wait_ge(ev("is0"), 1)
            V.tensor_tensor(code[:, :], etype, is0[:, :], ALU.add).then_inc(ev("code"), 1)
            dve.wait_ge(ev("code"), 1)
            dve.wait_ge(ev("digit"), 1)
            V.tensor_tensor(code[:, :], code[:, :], digit[:, :].bitcast(F32), ALU.mult).then_inc(ev("code"), 1)
            dve.wait_ge(ev("cols_loaded"), 16)
            affine_T((4, 5), lnT, "g1", "be1", "lnx_tr", "lnT")
            dve.wait_ge(ev("node_iota"), 1)
            iota_c = node_iota[:, :].unsqueeze(1).to_broadcast([P, EC, N])
            V.tensor_tensor(src_hot, iota_c, spread(esrc, N), ALU.is_equal).then_inc(ev("src_hot"), 1)
            V.tensor_tensor(dst_val[:, :, :], iota_c, spread(edst, N), ALU.is_equal).then_inc(ev("dst_hot"), 1)
            dve.wait_ge(ev("upper"), 1)
            dve.wait_ge(ev("keyc"), 1)
            for c in range(EC):
                if c % TPB == 0:
                    dve.wait_ge(ev("keys_ps"), c // TPB + 1)
                if c:
                    dve.wait_ge(ev("dup"), c)
                b = 6 + (c // TPB) % 2
                V.scalar_tensor_tensor(junk[:, :], bank[b][:, (c % TPB) * P:(c % TPB + 1) * P], keyc[:, c:c + 1],
                                       upper[:, :], ALU.is_equal, ALU.mult, accum_out=dup[:, c:c + 1])\
                    .then_inc(ev("dup"), 1)
            dve.wait_ge(ev("dup"), EC)
            V.scalar_tensor_tensor(code[:, :], dup[:, :], 0.0, code[:, :], ALU.is_equal, ALU.mult).then_inc(ev("code"), 1)
            dve.wait_ge(ev("code"), 3)
            dve.wait_ge(ev("dst_hot"), 1)
            V.tensor_tensor(dst_val[:, :, :], dst_val[:, :, :], spread(code[:, :], N), ALU.mult).then_inc(ev("dst_val"), 1)
            dve.wait_ge(ev("etw_ln"), 1)
            V.scalar_tensor_tensor(wmask[:, :], etw_sb[:, :], 0.0, sp_a[:, :], ALU.max, ALU.add).then_inc(ev("wmask"), 1)

            features(mkT, negT, expT, "mkT", "mk")
            dve.wait_ge(ev("mk_feat"), 1)
            V.tensor_reduce(z_sb[:, :], mkT[:, :, :], AX.X, ALU.add).then_inc(ev("z_sb"), 1)

            dve.wait_ge(ev("edge_ps"), 1)
            V.tensor_copy(esum[:, :], bank[6][0:N, 0:N]).then_inc(ev("esum"), 1)
            dve.wait_ge(ev("ident"), 1)
            V.tensor_scalar(ediag[:, :], ident[0:N, 0:N], 4.0, None, ALU.mult).then_inc(ev("ediag"), 1)
            V.tensor_scalar(far[:, :], ident[0:N, 0:N], FAR, -FAR, ALU.mult, ALU.add).then_inc(ev("far"), 1)
            dve.wait_ge(ev("esum"), 1)
            V.tensor_scalar(ecode[:, :], esum[:, :].bitcast(I32), 22, 7, ALU.logical_shift_right, ALU.bitwise_and)\
                .then_inc(ev("ecode"), 1)
            V.tensor_scalar(absent[:, :], esum[:, :], 0.0, None, ALU.is_equal).then_inc(ev("absent"), 1)
            dve.wait_ge(ev("absent"), 1)
            dve.wait_ge(ev("far"), 1)
            V.tensor_tensor(mtmp[:, :], absent[:, :], ediag[:, :], ALU.mult).then_inc(ev("mtmp"), 1)
            V.tensor_tensor(absent[:, :], absent[:, :], far[:, :], ALU.mult).then_inc(ev("absent"), 1)
            dve.wait_ge(ev("mtmp"), 1)
            dve.wait_ge(ev("ecode"), 1)
            V.tensor_tensor(ecodef[:, :], ecode[:, :], mtmp[:, :], ALU.add).then_inc(ev("ecodef"), 1)
            dve.wait_ge(ev("ecodef"), 1)
            dve.wait_ge(ev("wmask"), 1)
            prev = absent
            for i, c in enumerate((0, 2, 3, 4)):
                if i:
                    dve.wait_ge(ev("mask"), i)
                V.tensor_scalar(mtmp[:, :], ecodef[:, :], float(c), wmask[:, i:i + 1], ALU.is_equal, ALU.mult)\
                    .then_inc(ev("mtmp"), 1)
                dve.wait_ge(ev("mtmp"), 2 + i)
                dve.wait_ge(ev("absent"), 2)
                V.tensor_tensor(mask[:, :], prev[:, :], mtmp[:, :], ALU.add).then_inc(ev("mask"), 1)
                prev = mask

            def max_rhs(c):
                dve.wait_ge(ev(f"rhs_full{c % 2}"), 16 * (c // 2 + 1))
                V.tensor_reduce(ramax[:, c % 2, :], rhs_stage[:, c % 2, :].rearrange("p (k n) -> p n k", k=KT),
                                AX.X, ALU.max, apply_absolute_value=True).then_inc(ev("rhs_pmax"), 1)

            def scale_rhs(c):
                st = rhs_stage[:, c % 2, :].rearrange("p (k n) -> p k n", k=KT)
                dve.wait_ge(ev("rhs_amax"), c + 1)
                sc = rscale[:, c * 256:(c + 1) * 256]
                V.tensor_scalar(sc, ramax[:, c % 2, :], ABSMAX_FLOOR, 1.0 / INT8_MAX, ALU.max, ALU.mult)\
                    .then_inc(ev("rhs_scale"), 1)
                dve.wait_ge(ev("rhs_scale"), c + 1)
                V.reciprocal(rinv[:, c % 2, :], sc).then_inc(ev("rhs_inv"), 1)
                dve.wait_ge(ev("rhs_inv"), c + 1)
                V.tensor_tensor(st, st, rinv[:, c % 2, :].unsqueeze(1).to_broadcast([P, KT, 256]), ALU.mult)\
                    .then_inc(ev("rhs_div"), 1)
                dve.wait_ge(ev("rhs_div"), c + 1)
                V.tensor_scalar(st, st, INT8_MAX, -INT8_MAX, ALU.min, ALU.max).then_inc(ev("rhs_scaled"), 1)

            max_rhs(0)
            max_rhs(1)
            scale_rhs(0)
            features(mqT, negT, expT, "mqT", "mq")
            dve.wait_ge(ev("z_sb"), 1)
            dve.wait_ge(ev("blockm"), 2)
            V.tensor_tensor(kvz[:, 1, :, :], blockm[:, :].unsqueeze(1).to_broadcast([P, KT, P]),
                            spread(z_sb[:, :], P), ALU.mult).then_inc(ev("kv"), 1)
            for h in range(2):
                dve.wait_ge(ev("kv_ps"), h + 1)
                V.tensor_tensor(kvz[:, 0, TPB * h:TPB * (h + 1), :], bank[4 + h][:, :].rearrange("p (j n) -> p j n", j=TPB),
                                blockm[:, :].unsqueeze(1).to_broadcast([P, TPB, P]), ALU.mult).then_inc(ev("kv"), 1)
            scale_rhs(1)
            for h in range(2):
                js = slice(TPB * h, TPB * (h + 1))
                dve.wait_ge(ev("den_ps"), h + 1)
                V.tensor_scalar(negT[:, js, :], tiles(6 + h), ATTN_EPS, None, ALU.max).then_inc(ev("den"), 1)
            dve.wait_ge(ev("den"), 2)
            V.reciprocal(negT[:, :, :], negT[:, :, :]).then_inc(ev("rden"), 1)
            dve.wait_ge(ev("rden"), 1)
            for h in range(2):
                js = slice(TPB * h, TPB * (h + 1))
                V.tensor_tensor(yT[:, js, :], tiles(4 + h), negT[:, js, :], ALU.mult).then_inc(ev("yT"), 1)
            for c in (2, 3):
                max_rhs(c)
                scale_rhs(c)

            for h in range(2):
                js = slice(TPB * h, TPB * (h + 1))
                dve.wait_ge(ev("owT"), h + 1)
                V.tensor_tensor(y1T[:, js, :], xnT[:, js, :], owT[:, js, :], ALU.add).then_inc(ev("y1T"), 1)
            layer_norm(2, y1_rows[:, :], ln2_rows[:, :], "y1_rows", (1, 2))
            dve.wait_ge(ev("mask"), 4)

            def shift_scores(g):
                hs = group_heads(g)
                pg = probs[:, hs[0]:hs[-1] + 1:2, :]
                mx = smax[:, 4 * g:4 * g + 4]
                dve.wait_ge(ev("scores_ps"), g + 1)
                V.scalar_tensor_tensor(pg, tiles(4 + g)[0:N, :, :], float(HD) ** -0.5,
                                       mask[:, :].unsqueeze(1).to_broadcast([N, 4, N]), ALU.mult, ALU.add)\
                    .then_inc(ev("scores"), 1)
                dve.wait_ge(ev("scores"), g + 1)
                V.tensor_reduce(mx, pg, AX.X, ALU.max).then_inc(ev("smax"), 1)
                dve.wait_ge(ev("smax"), g + 1)
                V.tensor_tensor(pg, pg, spread(mx, N), ALU.subtract).then_inc(ev("scores_shifted"), 1)

            def normalise(g):
                hs = group_heads(g)
                pg = probs[:, hs[0]:hs[-1] + 1:2, :]
                sm = ssum[:, 4 * g:4 * g + 4]
                rs = rsum[:, 4 * g:4 * g + 4]
                dve.wait_ge(ev("probs_exp"), g + 1)
                V.tensor_reduce(sm, pg, AX.X, ALU.add).then_inc(ev("ssum"), 1)
                dve.wait_ge(ev("ssum"), g + 1)
                V.reciprocal(rs, sm).then_inc(ev("rsum"), 1)
                dve.wait_ge(ev("rsum"), g + 1)
                V.tensor_tensor(pg, pg, spread(rs, N), ALU.mult).then_inc(ev("probs"), 1)

            shift_scores(0)
            for g in range(1, 4):
                shift_scores(g)
                normalise(g - 1)
            normalise(3)
            for g in (0, 2):
                hs = group_heads(g)
                dve.wait_ge(ev("probs_tr"), g + 1)
                V.tensor_copy(probsT[:, hs[0]:hs[-1] + 1:2, :], tiles(4 + g)[0:N, :, :]).then_inc(ev("probsT_even"), 1)
            affine_T((2, 3), ln2T, "g2", "be2", "ln2_tr", "ln2T")

            dve.wait_ge(ev("base"), 1)
            mean = mv[:, 3, 0:1]
            for i, (b, c0, width) in enumerate(PIECES):
                cs = slice(c0, c0 + width)
                dve.wait_ge(ev("wo_ps"), i + 1)
                V.tensor_tensor(x1_rows[:, cs], bank[b][0:N, 0:width], base_rows[:, cs], ALU.add).then_inc(ev("x1"), 1)
                dve.wait_ge(ev("x1"), i + 1)
                for c in range(c0 // QUARTER, (c0 + width) // QUARTER):
                    V.bn_stats(stats_x1[:, c, :], x1_rows[:, c * QUARTER:(c + 1) * QUARTER]).then_inc(ev("bn_x1"), 1)
                V.tensor_reduce(extremes[:, 0, i:i + 1], x1_rows[:, cs], AX.X, ALU.max).then_inc(ev("x1_max"), 1)
                if i == 2:
                    dve.wait_ge(ev("bn_x1"), 4)
                    V.bn_aggr(mv[:, 3, :], stats_x1[:, :, :]).then_inc(ev("ln_stats"), 1)
                V.tensor_reduce(extremes[:, 1, i:i + 1], x1_rows[:, cs], AX.X, ALU.min).then_inc(ev("x1_min"), 1)
            amax, scale, qs, ls = (lscale[:, i:i + 1] for i in range(4))
            dve.wait_ge(ev("x1_min"), 3)
            dve.wait_ge(ev("ln_stats"), 4)
            V.tensor_scalar(extremes[:, 0, :], extremes[:, 0, :], mean, 1.0 / INT8_MAX, ALU.subtract, ALU.mult)\
                .then_inc(ev("spread"), 1)
            V.tensor_scalar(extremes[:, 1, :], extremes[:, 1, :], mean, -1.0 / INT8_MAX, ALU.subtract, ALU.mult)\
                .then_inc(ev("spread"), 1)
            dve.wait_ge(ev("spread"), 2)
            V.tensor_reduce(amax, extremes[:, :, :], AX.XY, ALU.max).then_inc(ev("lq"), 1)
            dve.wait_ge(ev("ln_sd"), 4)
            dve.wait_ge(ev("lq"), 1)
            V.scalar_tensor_tensor(scale, sd[:, 3:4], ABSMAX_FLOOR / INT8_MAX, amax, ALU.mult, ALU.max).then_inc(ev("lq"), 1)
            dve.wait_ge(ev("lq"), 2)
            V.reciprocal(qs, scale).then_inc(ev("lq"), 1)
            dve.wait_ge(ev("lq"), 3)
            for h in range(2):
                cs = slice(h * HALF, (h + 1) * HALF)
                V.tensor_scalar(xl_rows[:, cs], x1_rows[:, cs], mean, qs, ALU.subtract, ALU.mult).then_inc(ev("lq"), 1)
            for h in range(2):
                cs = slice(h * HALF, (h + 1) * HALF)
                dve.wait_ge(ev("lq"), 4 + h)
                V.tensor_scalar(xl_rows[:, cs], xl_rows[:, cs], ROUND, ROUND + INT8_MAX, ALU.add, ALU.min)\
                    .then_inc(ev("lq_magic"), 1)
            for h in range(2):
                cs = slice(h * HALF, (h + 1) * HALF)
                dve.wait_ge(ev("lq_magic"), h + 1)
                V.tensor_scalar(q_rows[:, cs], xl_rows[:, cs], ROUND - INT8_MAX, -ROUND, ALU.max, ALU.add)\
                    .then_inc(ev("q_rows"), 1)
            dve.wait_ge(ev("q8_tr"), 1)
            V.tensor_copy(q8T[:, 0:TPB, :], bank[4][:, 0:TPB * N // 2].bitcast(BF16)
                          .rearrange("p (j n) -> p j n", j=TPB)).then_inc(ev("q8T_a"), 1)
            V.reciprocal(rstd[:, 3:4], sd[:, 3:4]).then_inc(ev("ln_rstd"), 1)
            dve.wait_ge(ev("ln_rstd"), 4)
            V.tensor_tensor(ls, scale, rstd[:, 3:4], ALU.mult).then_inc(ev("ls"), 1)
            dve.wait_ge(ev("ls"), 1)
            V.tensor_scalar(xl_rows[:, :], rscale[0:N, :], ls, None, ALU.mult).then_inc(ev("scales"), 1)
            dve.wait_ge(ev("scales"), 1)
            for c in range(4):
                cs = slice(c * QUARTER, (c + 1) * QUARTER)
                dve.wait_ge(ev("ffn_ps"), c + 1)
                V.tensor_tensor(xl_rows[:, cs], bank[FFN_BANKS[c]][0:N, 0:QUARTER],
                                xl_rows[:, cs], ALU.mult).then_inc(ev("ffn"), 1)
                if c >= 2:
                    dve.wait_ge(ev("ffn"), c + 1)
                    V.tensor_tensor(x1_rows[:, cs], x1_rows[:, cs], xl_rows[:, cs], ALU.add).then_inc(ev("out_ready"), 1)

        @block.tensor
        def _(pe):
            T = nc.tensor

            def chunk_arrived(w, q):
                c = FIRST[w] + q
                pe.wait_ge(ev(f"slot_full{c % RING}"), 16 * (c // RING + 1))

            def project_T(w, src, banks, q):
                chunk_arrived(w, q)
                for j in (2 * q, 2 * q + 1):
                    for k in range(KT):
                        ins = T.matmul(tiles(banks[j // TPB])[:, j % TPB, :],
                                       slot(w, q)[:, ((j % 2) * KT + k) * P:((j % 2) * KT + k + 1) * P],
                                       src[:, k, :], start=(k == 0), stop=(k == KT - 1))
                ins.then_inc(ev("chunk_done"), 1)

            def rows_to_T(src, banks, name):
                for h in range(2):
                    for j in range(TPB * h, TPB * h + TPB):
                        ins = T.transpose(tiles(banks[h])[:, j % TPB, :], src[:, j * P:(j + 1) * P], ident[0:N, 0:N])
                    ins.then_inc(ev(name), 1)

            def T_to_rows(src, banks, name):
                for h in range(2):
                    for j in range(TPB * h, TPB * h + TPB):
                        ins = T.transpose(bank[banks[h]][0:N, (j % TPB) * P:(j % TPB + 1) * P], src[:, j, :], ident[:, :])
                    ins.then_inc(ev(name), 1)

            def keys(r):
                if r:
                    pe.wait_ge(ev("dup"), 8 * r)
                for b in range(2):
                    o = (2 * r + b) * HALF
                    T.matmul(bank[6 + b][:, :], keyw[:, :], keyrow[:, o:o + HALF], start=True, stop=True)\
                        .then_inc(ev("keys_ps"), 1)

            def warm_up(n):
                for _ in range(n):
                    T.matmul(bank[5][:, 0:P], ones[:, :], ones[:, :], start=True, stop=True)

            pe.wait_ge(ev("ones"), 1)
            warm_up(HEAD_WARM)
            pe.wait_ge(ev("ident"), 1)
            pe.wait_ge(ev("ln_done"), 1)
            rows_to_T(xn_rows, (0, 1), "xn_tr")

            pe.wait_ge(ev("xnT_a"), 1)
            pe.wait_ge(ev("xnT_b"), 1)
            project_T("q", xnT, (2, 3), 0)
            pe.wait_ge(ev("ln_done"), 2)
            rows_to_T(ln_rows, (4, 5), "lnx_tr")
            pe.wait_ge(ev("rowb_loaded"), 16)
            for h in range(2):
                T.matmul(bank[h][0:N, :], ones[0:2, 0:N], rowb[:, h * HALF:(h + 1) * HALF], start=True, stop=True)\
                    .then_inc(ev("rowbias_ps"), 1)
            project_T("q", xnT, (2, 3), 1)
            pe.wait_ge(ev("keyrow"), 1)
            pe.wait_ge(ev("keyw"), 1)
            keys(0)
            project_T("q", xnT, (2, 3), 2)
            project_T("q", xnT, (2, 3), 3)

            pe.wait_ge(ev("lnT"), 2)
            pe.wait_ge(ev("rowbias_out"), 2)
            project_T("mk", lnT, (0, 1), 0)
            keys(1)
            project_T("mk", lnT, (0, 1), 1)
            project_T("mk", lnT, (0, 1), 2)
            keys(2)
            project_T("mk", lnT, (0, 1), 3)

            pe.wait_ge(ev("qT"), 2)
            project_T("mv", lnT, (2, 3), 0)
            project_T("mv", lnT, (2, 3), 1)
            pe.wait_ge(ev("src_hot"), 1)
            pe.wait_ge(ev("dst_val"), 1)
            for c in range(EC):
                ins = T.matmul(bank[6][0:N, 0:N], src_hot[:, c, :], dst_val[:, c, :], start=(c == 0), stop=(c == EC - 1))
            ins.then_inc(ev("edge_ps"), 1)
            project_T("mv", lnT, (2, 3), 2)
            project_T("mv", lnT, (2, 3), 3)

            pe.wait_ge(ev("mkT"), 2)
            project_T("mq", lnT, (0, 1), 0)
            project_T("mq", lnT, (0, 1), 1)
            pe.wait_ge(ev("mk_feat"), 1)
            pe.wait_ge(ev("lnT"), 2)
            T_to_rows(mkT, (4, 5), "kf_tr")
            pe.wait_ge(ev("mvT"), 2)
            pe.wait_ge(ev("esum"), 1)
            T_to_rows(mvT, (6, 7), "mv_tr")
            project_T("mq", lnT, (0, 1), 2)
            project_T("mq", lnT, (0, 1), 3)

            project_T("k", xnT, (2, 3), 0)
            project_T("k", xnT, (2, 3), 1)
            pe.wait_ge(ev("kf_rows"), 2)
            pe.wait_ge(ev("mv_rows"), 2)
            for j in range(KT):
                js = slice(j * P, (j + 1) * P)
                ins = T.matmul(bank[4 + j // TPB][:, (j % TPB) * P:(j % TPB + 1) * P], kf_rows[:, js], mv_rows[:, js],
                               start=True, stop=True)
                if j % TPB == TPB - 1:
                    ins.then_inc(ev("kv_ps"), 1)
            project_T("k", xnT, (2, 3), 2)
            project_T("k", xnT, (2, 3), 3)

            pe.wait_ge(ev("mqT"), 2)
            project_T("v", xnT, (0, 1), 0)
            pe.wait_ge(ev("kv"), 3)
            pe.wait_ge(ev("mq_feat"), 1)
            for what in range(2):
                for j in range(KT):
                    ins = T.matmul(tiles(4 + 2 * what + j // TPB)[:, j % TPB, :], kvz[:, what, j, :], mqT[:, j, :],
                                   start=True, stop=True)
                    if what == 1 and j % TPB == TPB - 1:
                        ins.then_inc(ev("den_ps"), 1)
            for q in range(1, 4):
                project_T("v", xnT, (0, 1), q)

            pe.wait_ge(ev("kT"), 2)
            for q in range(4):
                project_T("q2", qT, (2, 3), q)
            pe.wait_ge(ev("vT"), 2)
            pe.wait_ge(ev("yT"), 2)
            for q in range(4):
                project_T("ow", yT, (0, 1), q)

            pe.wait_ge(ev("q2T"), 2)
            project_T("k2", kT, (2, 3), 0)
            pe.wait_ge(ev("y1T"), 2)
            T_to_rows(y1T, (4, 5), "y1_tr")
            for q in range(1, 4):
                project_T("k2", kT, (2, 3), q)

            def project_rows(w, src, banks, q, start):
                chunk_arrived(w, q)
                for k in (2 * q, 2 * q + 1):
                    for h in range(2):
                        ins = T.matmul(bank[banks[h]][0:N, :], src[:, k, :],
                                       slot(w, q)[:, (k % 2) * D + h * HALF:(k % 2) * D + (h + 1) * HALF],
                                       start=start and k == 0, stop=(k == KT - 1), skip_group_check=True)
                ins.then_inc(ev("chunk_done"), 1)

            pe.wait_ge(ev("owT"), 2)
            project_rows("v2", vT, (0, 1), 0, True)
            pe.wait_ge(ev("k2T"), 2)
            pe.wait_ge(ev("y1_rows"), 2)
            for g in range(4):
                for i, h in enumerate(group_heads(g)):
                    r = slice(HD * (h % 2), HD * (h % 2) + HD)
                    ins = T.matmul(tiles(4 + g)[0:N, i, :], q2T[r, h // 2, :], k2T[r, h // 2, :], start=True, stop=True)
                ins.then_inc(ev("scores_ps"), 1)
            pe.wait_ge(ev("ln_done"), 3)
            rows_to_T(ln2_rows, (2, 3), "ln2_tr")
            project_rows("v2", vT, (0, 1), 1, False)
            project_rows("v2", vT, (0, 1), 2, False)
            project_rows("v2", vT, (0, 1), 3, False)

            def turn_probs(g):
                pe.wait_ge(ev("probs"), g + 1)
                for i, h in enumerate(group_heads(g)):
                    ins = T.transpose(tiles(4 + g)[0:N, i, :], probs[:, h, :], ident[0:N, 0:N])
                ins.then_inc(ev("probs_tr"), 1)

            for g in range(4):
                turn_probs(g)
            pe.wait_ge(ev("v2_rows"), 2)
            for h in range(H):
                if h % 8 == 0:
                    pe.wait_ge(ev("probsT_even"), 1 + h // 8)
                    pe.wait_ge(ev("probsT_odd"), 1 + h // 8)
                r = slice(HD * (h % 2), HD * (h % 2) + HD)
                ins = T.matmul(tiles(h // 8)[r, (h % 8) // 2, :], v2_rows[:, h * HD:(h + 1) * HD], probsT[:, h, :],
                               start=True, stop=True)
                if h % 8 == 7:
                    ins.then_inc(ev("pv_ps"), 1)
            def wo_products(i, k):
                b, c0, width = PIECES[i]
                cs = slice((k % 2) * D + c0, (k % 2) * D + c0 + width)
                return T.matmul(bank[b][0:N, 0:width], aT[:, k, :], slot("wo", k // 2)[:, cs], start=(k == 0),
                                stop=(k == KT - 1), skip_group_check=True)

            pe.wait_ge(ev("aT"), 1)
            pe.wait_ge(ev("ln2T"), 2)
            chunk_arrived("wo", 0)
            for k in (0, 1):
                for i in range(3):
                    wo_products(i, k)
            chunk_arrived("w12", 0)
            w1 = slot("w12", 0)[:, 0:D]
            w2 = slot("w12", 0)[:, D:2 * D]
            for k in range(KT):
                ins = T.matmul(bank[6][:, 0:N], w1[:, k * P:(k + 1) * P], ln2T[:, k, :], start=(k == 0), stop=(k == KT - 1))
            ins.then_inc(ev("h_ps"), 1)
            chunk_arrived("wo", 1)
            for k in (2, 3):
                wo_products(0, k)
            pe.wait_ge(ev("hT"), 1)
            for b, c0, width in PIECES:
                T.matmul(bank[b][0:N, 0:width], hT[:, :], w2[:, c0:c0 + width], start=False, stop=False,
                         skip_group_check=True)
            pe.wait_ge(ev("aT"), 2)
            chunk_arrived("wo", 2)
            chunk_arrived("wo", 3)
            for i in range(3):
                for k in range(TPB if i == 0 else 2, KT):
                    ins = wo_products(i, k)
                ins.then_inc(ev("wo_ps"), 1)
            pe.wait_ge(ev("rhs_rounded"), 4)
            for _ in range(TAIL_WARM):
                T.matmul(bank[1][:, :], rhs_q[:, 0, 0:P], rhs_q[:, 0, 0:HALF], start=True, stop=True)

            pe.wait_ge(ev("identb"), 1)
            for h in range(2):
                pe.wait_ge(ev("q_rows"), h + 1)
                for j in range(TPB * h, TPB * h + TPB):
                    ins = T.transpose(bank[4 + h][:, 0:TPB * N // 2].bitcast(BF16)[:, (j % TPB) * N:(j % TPB + 1) * N],
                                      q_rows[:, j * P:(j + 1) * P], identb[0:N, 0:N])
                ins.then_inc(ev("q8_tr"), 1)
            for c, k0 in ((0, 0), (1, 0), (0, TPB), (1, TPB), (2, 0), (2, TPB), (3, 0), (3, TPB)):
                pe.wait_ge(ev("q8T_b" if k0 else "q8T_a"), 1)
                for k in range(k0, k0 + TPB):
                    ins = T.matmul(bank[FFN_BANKS[c]][0:N, 0:QUARTER], q8T[:, k, :],
                                   rhs_q[:, c, k * QUARTER:(k + 1) * QUARTER], start=(k == 0), stop=(k == KT - 1),
                                   skip_group_check=True)
                if k0:
                    ins.then_inc(ev("ffn_ps"), 1)


def kernel(**inputs):
    import numpy as np
    from concourse import bacc
    from concourse.bass_utils import run_bass_kernel_spmd

    a = {k: np.ascontiguousarray(v) for k, v in inputs.items()}
    g, m = "L0_gnn_", "L0_mix_"

    def blocks_T(w):
        return w.reshape(KT, P, 4, 2, P).transpose(2, 1, 3, 0, 4).reshape(4, P, CHUNK)

    def blocks_rows(w):
        return w.reshape(4, 2, P, D).transpose(0, 2, 1, 3).reshape(4, P, CHUNK)

    qkv = a[m + "qkv_w"]
    parts = {
        "q": blocks_T(a[g + "wq"].T), "k": blocks_T(a[g + "wk"].T), "v": blocks_T(a[g + "wv"].T),
        "q2": blocks_T(a[g + "wiq"].T), "k2": blocks_T(a[g + "wik"].T), "v2": blocks_rows(a[g + "wiv"].T),
        "mq": blocks_T(qkv[:, 0:D]), "mk": blocks_T(qkv[:, D:2 * D]), "mv": blocks_T(qkv[:, 2 * D:3 * D]),
        "ow": blocks_T(a[m + "out_w"]), "wo": blocks_rows(a[g + "wo"].T),
        "w12": np.concatenate([a[m + "w1"].reshape(KT, P, P).transpose(1, 0, 2).reshape(P, D), a[m + "w2"]], axis=1)[None],
    }
    weights = np.ascontiguousarray(np.concatenate([parts[w] for w in ORDER]))
    vectors = {
        "bq": a[g + "bq"], "bk": a[g + "bk"], "bv": a[g + "bv"], "biq": a[g + "biq"], "bik": a[g + "bik"],
        "biv": a[g + "biv"], "mqb": a[m + "qkv_b"][0:D], "mkb": a[m + "qkv_b"][D:2 * D], "mvb": a[m + "qkv_b"][2 * D:],
        "outb": a[m + "out_b"], "g1": a[m + "g1"], "be1": a[m + "be1"], "g2": a[m + "g2"], "be2": a[m + "be2"],
    }
    arrays = {
        "x_in": a["x"],
        "weights": weights,
        "rhs": np.ascontiguousarray(a["L0_ffn_rhs"].reshape(KT, P, 4, 256).transpose(2, 1, 0, 3).reshape(4, P, CHUNK)),
        "cols": np.ascontiguousarray(np.concatenate([vectors[n].reshape(KT, P).T for n in COLS] + [a[m + "b1"][:, None]], axis=1)),
        "rowbias": np.ascontiguousarray(np.stack([a[g + "bo"], a[m + "b2"]])),
        "edge_cols": np.ascontiguousarray(np.stack([a[n].reshape(EC, P).T for n in ("src", "dst", "edge_type_5")], axis=1)),
        "edge_rows": np.ascontiguousarray(np.stack([a["src"], a["dst"]])),
        "etw": np.ascontiguousarray(np.broadcast_to(a[g + "edge_type_weights"], (N, 4))),
    }
    nc = bacc.Bacc("TRN2", target_bir_lowering=False, num_devices=1)
    aps = [nc.dram_tensor(n, v.shape, mybir.dt.from_np(v.dtype), kind="ExternalInput").ap() for n, v in arrays.items()]
    out = nc.dram_tensor("out_rows", (N, D), F32, kind="ExternalOutput").ap()
    build(nc, *aps, out)
    r = run_bass_kernel_spmd(nc, [arrays], core_ids=[0])
    return r.results[0]["out_rows"]
```

```python
from contextlib import ExitStack

import concourse.bass as bass
from concourse import mybir

F32 = mybir.dt.float32
BF16 = mybir.dt.bfloat16
F32R = mybir.dt.float32r
I32 = mybir.dt.int32
ALU = mybir.AluOpType
ACT = mybir.ActivationFunctionType
AX = mybir.AxisListType

P = 128
N = 96
D = 1024
KT = D // P
H = 16
HD = D // H
E = 3072
EC = E // P
HALF = 512
QUARTER = 256
PIECES = tuple((b, c * QUARTER, QUARTER) for c, b in enumerate((2, 3, 0, 1)))
FFN_BANKS = (6, 7, 2, 3)
TPB = KT // 2
LN_EPS = 1e-5
ATTN_EPS = 1e-6
ABSMAX_FLOOR = 1e-12
INT8_MAX = 127.0
ROUND = 1.5 * 2.0 ** 23
FAR = 1e30
DIGIT = 4
DIGIT0 = 80

ORDER = ["q", "mk", "mq", "mv", "k", "q2", "k2", "v", "ow", "v2", "w12", "wo"]
CHUNK = 2 * D
RING = 5
SPLIT = ["mk", "mv", "ow", "v2", "wo"]
UNIT0 = {w: KT * i for i, w in enumerate(SPLIT)}
UNITS = KT * len(SPLIT)
PART_BUFS = 5
PIECE_UNITS = 4
POOL_UNITS = (0, 2, 4, 6, 8, 10, 12, 14, 16, 17, 23, 26, 29, 32, 35)
HEAD_WARM = 12
TAIL_WARM = 24
FIRST = {}
_n = 0
for _w in ORDER:
    FIRST[_w] = _n
    _n += 1 if _w == "w12" else 4
CHUNKS = _n

COLS = ["bq", "bk", "bv", "biq", "bik", "biv", "mqb", "g1", "be1", "g2", "be2"]
COL = {name: KT * i for i, name in enumerate(COLS)}
COL_B1 = KT * len(COLS)
NCOLS = COL_B1 + 1


def build(nc, x, weights, rhs, cols, row_vectors, edge_cols, edge_rows, etw, out):
    assert CHUNKS % RING == 0
    with ExitStack() as ctx:
        sems = {}

        def ev(name):
            if name not in sems:
                sems[name] = ctx.enter_context(nc.semaphore(name))
            return sems[name]

        def sb(name, shape, dt=F32):
            return ctx.enter_context(nc.sbuf_tensor(name, shape, dt))

        ring = sb("ring", [P, RING, CHUNK])
        w_hi = sb("w_hi", [P, PART_BUFS, D], F32R)
        w_lo = sb("w_lo", [P, PART_BUFS, D], F32R)
        y_parts = sb("y_parts", [P, KT, 2, P], F32R)
        v_parts = sb("v_parts", [P, KT, 2, P], F32R)
        rhs_stage = sb("rhs_stage", [P, 2, CHUNK])
        rhs_q = sb("rhs_q", [P, 4, CHUNK], BF16)
        x_rows = sb("x_rows", [N, D])
        xn_rows = sb("xn_rows", [N, D])
        ln_rows = sb("ln_rows", [N, D])
        xnT = sb("xnT", [P, KT, N])
        lnT = sb("lnT", [P, KT, N])
        qT = sb("qT", [P, KT, N])
        kT = sb("kT", [P, KT, N])
        mqT = sb("mqT", [P, KT, N])
        yT = sb("yT", [P, KT, N])
        mvb_sb = sb("mvb_sb", [N, D])
        negT = sb("negT", [P, KT, N])
        expT = sb("expT", [P, KT, N])
        kvz = sb("kvz", [P, 2, KT, P])
        late = sb("late", [P, E // 2 + EC * N // 2])
        cols_sb = sb("cols_sb", [P, NCOLS])
        hT = sb("hT", [P, N])
        ident = sb("ident", [P, P])
        identb = sb("identb", [P, P], BF16)
        upper = sb("upper", [P, P])
        blockm = sb("blockm", [P, P])
        ones = sb("ones", [P, P])
        keyw = sb("keyw", [2, P], BF16)
        node_iota = sb("node_iota", [P, N])
        digit_exp = sb("digit_exp", [P, EC], I32)
        digit = sb("digit", [P, EC], I32)
        edge_i = sb("edge_i", [P, 3, EC], I32)
        edge_f = sb("edge_f", [P, 3, EC])
        keyc = sb("keyc", [P, EC])
        dup = sb("dup", [P, EC])
        code = sb("code", [P, EC])
        is0 = sb("is0", [P, EC])
        junk = sb("junk", [P, P])
        etw_sb = sb("etw_sb", [N, 4])
        sp_a = sb("sp_a", [N, 4])
        sp_b = sb("sp_b", [N, 4])
        wmask = sb("wmask", [N, 4])
        ediag = sb("ediag", [N, N])
        far = sb("far", [N, N])
        esum = sb("esum", [N, N])
        ecode = sb("ecode", [N, N], I32)
        ecodef = sb("ecodef", [N, N])
        absent = sb("absent", [N, N])
        mask = sb("mask", [N, N])
        mtmp = sb("mtmp", [N, N])
        z_sb = sb("z_sb", [P, KT])
        stats = sb("stats", [N, 3, 2, 6])
        stats_x1 = sb("stats_x1", [N, 4, 6])
        mv = sb("mv", [N, 4, 2])
        extremes = sb("extremes", [N, 2, 4])
        sd = sb("sd", [N, 4])
        rstd = sb("rstd", [N, 4])
        smax = sb("smax", [N, H])
        ssum = sb("ssum", [N, H])
        rsum = sb("rsum", [N, H])
        lscale = sb("lscale", [N, 4])
        ramax = sb("ramax", [P, 2, 256])
        rinv = sb("rinv", [P, 2, 256])
        rscale = sb("rscale", [P, D])
        q8T = sb("q8T", [P, KT, N], BF16)
        eps = sb("eps", [N, 1])
        warm = sb("warm", [N, 4])

        kf_rows, mv_rows = ln_rows, late[0:N, 0:D]
        vT, ln_parts = lnT, y_parts
        q2T, k2T, aT = mqT, negT, vT
        a_parts = v_parts
        y1_rows = kf_rows
        mvb_rows = mvb_sb[:, :]
        kf_neg, kf_exp = (kvz[0:N, i, :, :].rearrange("p a b -> p (a b)") for i in range(2))
        probs = kvz[:, :, :, :].rearrange("p a b c -> p (a b c)")[0:N, 0:H * N].rearrange("p (h n) -> p h n", h=H)
        x1_rows, xl_rows = xn_rows, ln_rows
        q_rows = late[0:N, 0:D // 2].bitcast(BF16)
        probsT = late[0:N, 0:H * N].rearrange("p (h n) -> p h n", h=H)
        v2_rows = late[0:N, H * N:H * N + D]
        keyrow = late[0:2, 0:E // 2].bitcast(BF16)
        src_hot = late[:, E // 2:E // 2 + EC * N // 2].bitcast(BF16).rearrange("p (c n) -> p c n", c=EC)
        dst_val = rhs_stage[:, 0, 0:EC * N // 2].bitcast(BF16).rearrange("p (c n) -> p c n", c=EC)
        mkb_rows = rhs_stage[0:N, 1, 0:D]
        bo_rows, b2_rows = (rhs_stage[0:N, 0, i * D:(i + 1) * D] for i in range(2))
        outb_rows = rhs_stage[0:N, 1, 0:D]
        base_rows, ln2_rows, ln2T = x_rows, bo_rows, lnT
        edge_row_i = rhs_q[:, :, :].rearrange("p a b -> p (a b)")[0:2, 0:2 * E].bitcast(I32)

        bank = [ctx.enter_context(nc.psum_tensor(f"bank{i}", [P, HALF], F32)) for i in range(8)]

        def slot(w, q):
            return ring[:, (FIRST[w] + q) % RING, :]

        def unit(u):
            return slot(SPLIT[u // KT], (u % KT) // 2)[:, (u % 2) * D:(u % 2 + 1) * D]

        def low_count(u):
            return sum((i in POOL_UNITS) == (u in POOL_UNITS) for i in range(u + 1))

        def chunk_count(w, q):
            return FIRST[w] + q + 1

        def tiles(b):
            return bank[b][:, 0:TPB * N].rearrange("p (j n) -> p j n", j=TPB)

        def col(name, j0, j1):
            return cols_sb[:, COL[name] + j0:COL[name] + j1]

        def spread(ap, n):
            return ap.unsqueeze(2).to_broadcast([ap.shape[0], ap.shape[1], n])

        def group_heads(g):
            return range(8 * (g // 2) + g % 2, 8 * (g // 2) + 8, 2)

        block = ctx.enter_context(nc.Block())

        @block.sync
        def _(sp):
            sp.dma_start(x_rows[:, :], x).then_inc(ev("x_loaded"), 16)
            sp.dma_start(cols_sb[:, :], cols).then_inc(ev("cols_loaded"), 16)
            sp.dma_start(etw_sb[:, :], etw).then_inc(ev("etw_loaded"), 16)
            for s in range(RING):
                sp.dma_start(ring[:, s, :], weights[s]).then_inc(ev(f"slot_full{s}"), 16)
            with sp.Fori(1, CHUNKS // RING) as r:
                for s in range(RING):
                    sp.wait_ge(ev("chunk_done"), r * RING + (s + 1 - RING))
                    sp.dma_start(ring[:, s, :], weights[bass.ds(r * RING + s, 1)].rearrange("a p n -> (a p) n"))\
                        .then_inc(ev(f"slot_full{s}"), 16)
            for c in range(4):
                cs = slice(c * QUARTER, (c + 1) * QUARTER)
                if c < 2:
                    sp.wait_ge(ev("out_ready_pool"), c + 1)
                else:
                    sp.wait_ge(ev("out_ready"), c - 1)
                sp.dma_start(out[:, cs], x1_rows[:, cs]).then_inc(ev("out_stored"), 16)
            sp.wait_ge(ev("out_stored"), 64)

        @block.gpsimd
        def _(pool):
            pool.memset(ident[:, :], 0.0).then_inc(ev("zeros"), 1)
            pool.memset(identb[:, :], 0.0).then_inc(ev("zeros"), 1)
            pool.memset(upper[:, :], 1.0).then_inc(ev("zeros"), 1)
            pool.wait_ge(ev("zeros"), 3)
            pool.affine_select(out=ident[:, :], in_=ident[:, :], compare_op=ALU.not_equal, fill=1.0, base=0,
                               pattern=[[-1, P]], channel_multiplier=1).then_inc(ev("ident"), 1)
            pool.affine_select(out=identb[:, :], in_=identb[:, :], compare_op=ALU.not_equal, fill=1.0, base=0,
                               pattern=[[-1, P]], channel_multiplier=1).then_inc(ev("identb"), 1)
            pool.affine_select(out=upper[:, :], in_=upper[:, :], compare_op=ALU.is_ge, fill=0.0, base=-1,
                               pattern=[[1, P]], channel_multiplier=-1).then_inc(ev("upper"), 1)
            pool.iota(node_iota[:, :], [[1, N]], base=0, channel_multiplier=0,
                      allow_small_or_imprecise_dtypes=True).then_inc(ev("node_iota"), 1)
            pool.iota(digit_exp[:, :], [[DIGIT, EC]], base=DIGIT0, channel_multiplier=0).then_inc(ev("digit_exp"), 1)
            pool.wait_ge(ev("edge_cols_loaded"), 16)
            pool.tensor_copy(edge_f[:, :, :], edge_i[:, :, :]).then_inc(ev("edge_f"), 1)

            def low_weights(u0, u1):
                for u in range(u0, u1):
                    if u in POOL_UNITS:
                        pool.wait_ge(ev("w_high"), u + 1)
                        pool.tensor_tensor(w_lo[:, u % PART_BUFS, :], unit(u), w_hi[:, u % PART_BUFS, :], ALU.subtract)\
                            .then_inc(ev("w_low_pool"), 1)

            pool.wait_ge(ev("ln_high"), 1)
            pool.tensor_tensor(ln_parts[:, :, 1, 0:N], lnT[:, :, :], ln_parts[:, :, 0, 0:N], ALU.subtract)\
                .then_inc(ev("ln_low"), 1)
            low_weights(0, UNIT0["ow"])
            pool.wait_ge(ev("edge_ps"), 1)
            pool.dma_start(rhs_stage[:, 0, :], rhs[0]).then_inc(ev("rhs_full0"), 16)
            pool.wait_ge(ev("kf_rows"), 2)
            pool.dma_start(rhs_stage[:, 1, :], rhs[1]).then_inc(ev("rhs_full1"), 16)
            for c in range(4):
                pool.wait_ge(ev("rhs_pmax"), c + 1)
                pool.partition_all_reduce(ramax[:, c % 2, :], ramax[:, c % 2, :], P,
                                          bass.bass_isa.ReduceOp.max).then_inc(ev("rhs_amax"), 1)
                if c == 1:
                    for i in range(2):
                        pool.wait_ge(ev("rhs_rounded"), i + 1)
                        pool.dma_start(rhs_stage[:, i, :], rhs[2 + i]).then_inc(ev(f"rhs_full{i}"), 16)
            pool.wait_ge(ev("y_high"), 1)
            pool.tensor_tensor(y_parts[:, :, 1, 0:N], yT[:, :, :], y_parts[:, :, 0, 0:N], ALU.subtract)\
                .then_inc(ev("y_low"), 1)
            pool.wait_ge(ev("rhs_rounded"), 4)
            for i, dst in enumerate((bo_rows, b2_rows, outb_rows)):
                pool.dma_start(dst, row_vectors[2 + i]).then_inc(ev("row_vectors_loaded"), 16)
            u0, u1, u2 = (UNIT0[w] for w in ("ow", "v2", "wo"))
            low_weights(u0, u0 + 2)
            pool.wait_ge(ev("row_vectors_loaded"), 48)
            pool.wait_ge(ev("ln_done"), 2)
            pool.tensor_tensor(xn_rows[:, :], xn_rows[:, :], outb_rows, ALU.add).then_inc(ev("xn_outb"), 1)
            pool.wait_ge(ev("v_high"), 1)
            pool.tensor_tensor(v_parts[:, :, 1, 0:N], vT[:, :, :], v_parts[:, :, 0, 0:N], ALU.subtract)\
                .then_inc(ev("v_low"), 1)
            low_weights(u0 + 2, u1)
            pool.tensor_tensor(base_rows[:, :], x_rows[:, :], bo_rows, ALU.add).then_inc(ev("base"), 1)
            low_weights(u1, u1 + 4)
            pool.wait_ge(ev("base"), 1)
            pool.tensor_tensor(base_rows[:, :], base_rows[:, :], b2_rows, ALU.add).then_inc(ev("base"), 1)
            low_weights(u1 + 4, u2 - 1)
            pool.wait_ge(ev("base"), 2)
            pool.wait_ge(ev("y1_rows"), 2)
            pool.tensor_tensor(base_rows[:, :], base_rows[:, :], y1_rows[:, :], ALU.add).then_inc(ev("base"), 1)
            low_weights(u2 - 1, UNITS)
            for c in range(2):
                cs = slice(c * QUARTER, (c + 1) * QUARTER)
                pool.wait_ge(ev("ffn"), c + 1)
                pool.tensor_tensor(x1_rows[:, cs], x1_rows[:, cs], xl_rows[:, cs], ALU.add).then_inc(ev("out_ready_pool"), 1)

        @block.scalar
        def _(act):
            A = nc.scalar
            act.wait_ge(ev("eps_set"), 1)
            A.activation(warm[:, 0:1], eps[:, :], ACT.Sqrt).then_inc(ev("warm"), 1)
            act.dma_start(edge_i[:, :, :], edge_cols).then_inc(ev("edge_cols_loaded"), 16)
            act.dma_start(edge_row_i, edge_rows).then_inc(ev("edge_rows_loaded"), 16)

            def deviation(i):
                act.wait_ge(ev("ln_stats"), i + 1)
                A.activation(sd[:, i:i + 1], mv[:, i, 1:2], ACT.Sqrt, bias=eps[:, :]).then_inc(ev("ln_sd"), 1)

            def add_bias(banks, h, dst, bias, name):
                for j in range(TPB * h, TPB * h + TPB):
                    ins = A.activation(dst[:, j, :], tiles(banks[h])[:, j % TPB, :], ACT.Identity,
                                       bias=col(bias, j, j + 1))
                ins.then_inc(ev(name), 1)

            def drain_T(w, banks, dst, bias, name):
                for h in range(2):
                    act.wait_ge(ev("chunk_done"), chunk_count(w, 2 * h + 1))
                    add_bias(banks, h, dst, bias, name)

            def high_weights(u0, u1):
                for u in range(u0, u1):
                    c = FIRST[SPLIT[u // KT]] + (u % KT) // 2
                    act.wait_ge(ev(f"slot_full{c % RING}"), 16 * (c // RING + 1))
                    last = u - PART_BUFS
                    if last >= 0 and last % 2 == 0:
                        act.wait_ge(ev("half_done"), last // 2 + 1)
                    if last >= 0 and last % 2 == 1:
                        act.wait_ge(ev("chunk_done"), chunk_count(SPLIT[last // KT], (last % KT) // 2))
                    A.activation(w_hi[:, u % PART_BUFS, :], unit(u), ACT.Copy).then_inc(ev("w_high"), 1)

            def round_rhs(c):
                act.wait_ge(ev("rhs_scaled"), c + 1)
                st = rhs_stage[:, c % 2, :]
                A.activation(st, st, ACT.Copy, bias=ROUND).then_inc(ev("rhs_magic"), 1)
                act.wait_ge(ev("rhs_magic"), c + 1)
                A.activation(rhs_q[:, c, :], st, ACT.Copy, bias=-ROUND).then_inc(ev("rhs_rounded"), 1)

            deviation(0)
            act.wait_ge(ev("xn_tr"), 1)
            A.activation(xnT[:, 0:TPB, :], tiles(0), ACT.Copy).then_inc(ev("xnT_a"), 1)
            deviation(1)
            act.wait_ge(ev("edge_rows_loaded"), 16)
            A.activation(keyrow, edge_row_i, ACT.Copy).then_inc(ev("keyrow"), 1)
            act.wait_ge(ev("etw_loaded"), 16)
            A.activation(sp_a[:, :], etw_sb[:, :], ACT.Abs).then_inc(ev("etw_abs"), 1)
            act.wait_ge(ev("etw_abs"), 1)
            A.activation(sp_b[:, :], sp_a[:, :], ACT.Exp, scale=-1.0).then_inc(ev("etw_exp"), 1)
            act.wait_ge(ev("etw_exp"), 1)
            A.activation(sp_a[:, :], sp_b[:, :], ACT.Ln, bias=1.0).then_inc(ev("etw_ln"), 1)
            act.wait_ge(ev("cols_loaded"), 16)
            act.wait_ge(ev("lnT"), 2)
            act.wait_ge(ev("padding"), 2)
            A.activation(ln_parts[:, :, 0, 0:N], lnT[:, :, :], ACT.Copy).then_inc(ev("ln_high"), 1)
            act.wait_ge(ev("chunk_done"), chunk_count("q", 1))
            add_bias((2, 3), 0, qT, "bq", "qT")
            high_weights(0, 5)
            act.wait_ge(ev("chunk_done"), chunk_count("q", 3))
            add_bias((2, 3), 1, qT, "bq", "qT")
            high_weights(5, 8)
            act.dma_start(mkb_rows, row_vectors[0]).then_inc(ev("mk_bias_loaded"), 16)
            act.dma_start(mvb_rows, row_vectors[1]).then_inc(ev("mv_bias_loaded"), 16)
            act.wait_ge(ev("mk_neg"), 1)
            A.activation(kf_exp, kf_neg, ACT.Exp).then_inc(ev("mk_exp"), 1)
            act.wait_ge(ev("chunk_done"), chunk_count("mq", 1))
            add_bias((2, 3), 0, mqT, "mqb", "mqT")
            high_weights(8, 13)
            act.wait_ge(ev("chunk_done"), chunk_count("mq", 3))
            add_bias((2, 3), 1, mqT, "mqb", "mqT")
            high_weights(13, 16)
            act.wait_ge(ev("mq_neg"), 1)
            A.activation(expT[:, :, :], negT[:, :, :], ACT.Exp).then_inc(ev("mq_exp"), 1)
            drain_T("k", (2, 3), kT, "bk", "kT")
            round_rhs(0)
            round_rhs(1)
            drain_T("q2", (0, 1), q2T, "biq", "q2T")
            act.wait_ge(ev("yT"), 2)
            A.activation(y_parts[:, :, 0, 0:N], yT[:, :, :], ACT.Copy).then_inc(ev("y_high"), 1)
            drain_T("k2", (2, 3), k2T, "bik", "k2T")
            round_rhs(2)
            round_rhs(3)
            for g in range(4):
                act.wait_ge(ev("scores_shifted"), g + 1)
                hs = group_heads(g)
                pg = probs[:, hs[0]:hs[-1] + 1:2, :]
                A.activation(pg, pg, ACT.Exp).then_inc(ev("probs_exp"), 1)
                if g == 1:
                    act.wait_ge(ev("chunk_done"), chunk_count("v", 1))
                    add_bias((0, 1), 0, vT, "bv", "vT")
                    high_weights(16, 17)
                if g == 2:
                    high_weights(17, 18)
                if g == 3:
                    high_weights(18, 19)
                    A.activation(warm[:, 3:4], eps[:, :], ACT.Sqrt).then_inc(ev("warm"), 1)
                    high_weights(19, 20)
            act.wait_ge(ev("chunk_done"), chunk_count("v", 3))
            add_bias((0, 1), 1, vT, "bv", "vT")
            high_weights(20, 21)
            act.wait_ge(ev("vT"), 2)
            A.activation(v_parts[:, :, 0, 0:N], vT[:, :, :], ACT.Copy).then_inc(ev("v_high"), 1)
            high_weights(21, 22)
            high_weights(22, 24)
            for g in (1, 3):
                hs = group_heads(g)
                act.wait_ge(ev("probs_tr"), g + 1)
                A.activation(probsT[:, hs[0]:hs[-1] + 1:2, :], tiles(4 + g)[0:N, :, :], ACT.Copy)\
                    .then_inc(ev("probsT_odd"), 1)
            high_weights(24, 27)
            high_weights(27, 30)
            deviation(2)
            high_weights(30, 32)
            A.activation(warm[:, 1:2], eps[:, :], ACT.Gelu).then_inc(ev("warm"), 1)
            high_weights(32, 35)
            act.wait_ge(ev("chunk_done"), chunk_count("v2", 3))
            for h in range(2):
                A.activation(v2_rows[:, h * HALF:(h + 1) * HALF], bank[h][0:N, :], ACT.Copy).then_inc(ev("v2_rows"), 1)
            high_weights(35, 36)
            act.wait_ge(ev("h_ps"), 1)
            A.activation(hT[:, :], bank[6][:, 0:N], ACT.Gelu, bias=cols_sb[:, COL_B1:COL_B1 + 1]).then_inc(ev("hT"), 1)
            act.wait_ge(ev("pv_ps"), 2)
            add_bias((4, 5), 1, aT, "biv", "aT")
            act.wait_ge(ev("aT"), 1)
            A.activation(a_parts[:, TPB:KT, 0, 0:N], aT[:, TPB:KT, :], ACT.Copy).then_inc(ev("a_high"), 1)
            high_weights(36, 40)
            A.activation(warm[:, 2:3], eps[:, :], ACT.Sqrt).then_inc(ev("warm"), 1)
            deviation(3)
            act.wait_ge(ev("q8_tr"), 2)
            A.activation(q8T[:, TPB:KT, :], bank[5][:, 0:TPB * N // 2].bitcast(BF16)
                         .rearrange("p (j n) -> p j n", j=TPB), ACT.Copy).then_inc(ev("q8T_b"), 1)

        @block.vector
        def _(dve):
            V = nc.vector

            def norm_stats(i, h, src):
                V.bn_stats(stats[:, i, h, :], src[:, h * HALF:(h + 1) * HALF]).then_inc(ev("bn"), 1)

            def norm_mean(i):
                dve.wait_ge(ev("bn"), 2 * i + 2)
                V.bn_aggr(mv[:, i, :], stats[:, i, :, :]).then_inc(ev("ln_stats"), 1)

            def norm_rstd(i):
                dve.wait_ge(ev("ln_sd"), i + 1)
                V.reciprocal(rstd[:, i:i + 1], sd[:, i:i + 1]).then_inc(ev("ln_rstd"), 1)
                dve.wait_ge(ev("ln_rstd"), i + 1)

            def layer_norm(i, src, dst, ready, values):
                for h in range(2):
                    dve.wait_ge(ev(ready), values[h])
                    norm_stats(i, h, src)
                norm_mean(i)
                norm_rstd(i)
                V.tensor_scalar(dst, src, mv[:, i, 0:1], rstd[:, i:i + 1], ALU.subtract, ALU.mult)\
                    .then_inc(ev("ln_done"), 1)

            def affine_T(banks, dst, g, b, ps_ready, name):
                for h in range(2):
                    js = slice(TPB * h, TPB * (h + 1))
                    dve.wait_ge(ev(ps_ready), h + 1)
                    V.tensor_tensor(dst[:, js, :], tiles(banks[h]), spread(col(g, js.start, js.stop), N), ALU.mult)\
                        .then_inc(ev(name + "_g"), 1)
                    dve.wait_ge(ev(name + "_g"), h + 1)
                    V.tensor_tensor(dst[:, js, :], dst[:, js, :], spread(col(b, js.start, js.stop), N), ALU.add)\
                        .then_inc(ev(name), 1)

            def low_weights(u0, u1):
                for u in range(u0, u1):
                    if u not in POOL_UNITS:
                        dve.wait_ge(ev("w_high"), u + 1)
                        V.tensor_tensor(w_lo[:, u % PART_BUFS, :], unit(u), w_hi[:, u % PART_BUFS, :], ALU.subtract)\
                            .then_inc(ev("w_low_dve"), 1)

            def rows_plus_bias(w, banks, bias, dst, name):
                dve.wait_ge(ev(w + "_bias_loaded"), 16)
                for h in range(2):
                    cs = slice(h * HALF, (h + 1) * HALF)
                    dve.wait_ge(ev("chunk_done"), chunk_count(w, 3))
                    V.tensor_tensor(dst[:, cs], bank[banks[h]][0:N, :], bias[:, cs], ALU.add).then_inc(ev(name), 1)

            def features_begin(src, neg, ready, name):
                dve.wait_ge(ev(ready), 2)
                V.tensor_scalar(neg, src, 0.0, None, ALU.min).then_inc(ev(name + "_neg"), 1)

            def features_end(src, exp, name):
                dve.wait_ge(ev(name + "_exp"), 1)
                V.scalar_tensor_tensor(src, src, 0.0, exp, ALU.max, ALU.add).then_inc(ev(name + "_feat"), 1)

            V.memset(eps[:, :], LN_EPS).then_inc(ev("eps_set"), 1)
            V.memset(ones[:, :], 1.0).then_inc(ev("ones"), 1)
            V.memset(keyw[:, :], 1.0).then_inc(ev("keyw0"), 1)
            V.memset(blockm[:, :], 0.0).then_inc(ev("blockm0"), 1)
            dve.wait_ge(ev("keyw0"), 1)
            V.memset(keyw[0:1, :], float(P)).then_inc(ev("keyw"), 1)
            dve.wait_ge(ev("blockm0"), 1)
            V.memset(blockm[0:HD, 0:HD], 1.0).then_inc(ev("blockm"), 1)
            V.memset(blockm[HD:P, HD:P], 1.0).then_inc(ev("blockm"), 1)

            layer_norm(0, x_rows[:, :], xn_rows[:, :], "x_loaded", (16, 16))
            dve.wait_ge(ev("ln_done"), 1)
            norm_stats(1, 0, xn_rows)
            dve.wait_ge(ev("xn_tr"), 2)
            V.tensor_copy(xnT[:, TPB:KT, :], tiles(1)).then_inc(ev("xnT_b"), 1)
            norm_stats(1, 1, xn_rows)
            norm_mean(1)
            norm_rstd(1)
            V.tensor_scalar(ln_rows[:, :], xn_rows[:, :], mv[:, 1, 0:1], rstd[:, 1:2], ALU.subtract, ALU.mult)\
                .then_inc(ev("ln_done"), 1)

            dve.wait_ge(ev("ones"), 1)
            for parts in (y_parts, v_parts):
                V.tensor_scalar(parts[:, :, :, :].rearrange("p k s n -> p (k s) n")[:, :, N:P],
                                ones[:, N:P].unsqueeze(1).to_broadcast([P, 2 * KT, P - N]), 0.0, None, ALU.mult)\
                    .then_inc(ev("padding"), 1)

            dve.wait_ge(ev("edge_f"), 1)
            esrc, edst, etype = (edge_f[:, i, :] for i in range(3))
            V.scalar_tensor_tensor(keyc[:, :], esrc, float(P), edst, ALU.mult, ALU.add).then_inc(ev("keyc"), 1)
            V.tensor_scalar(is0[:, :], etype, 0.0, 4.0, ALU.is_equal, ALU.mult).then_inc(ev("is0"), 1)
            dve.wait_ge(ev("digit_exp"), 1)
            V.tensor_scalar(digit[:, :], digit_exp[:, :], 23, None, ALU.logical_shift_left).then_inc(ev("digit"), 1)
            dve.wait_ge(ev("is0"), 1)
            V.tensor_tensor(code[:, :], etype, is0[:, :], ALU.add).then_inc(ev("code"), 1)
            dve.wait_ge(ev("code"), 1)
            dve.wait_ge(ev("digit"), 1)
            V.tensor_tensor(code[:, :], code[:, :], digit[:, :].bitcast(F32), ALU.mult).then_inc(ev("code"), 1)
            dve.wait_ge(ev("cols_loaded"), 16)
            affine_T((4, 5), lnT, "g1", "be1", "lnx_tr", "lnT")
            dve.wait_ge(ev("node_iota"), 1)
            iota_c = node_iota[:, :].unsqueeze(1).to_broadcast([P, EC, N])
            V.tensor_tensor(src_hot, iota_c, spread(esrc, N), ALU.is_equal).then_inc(ev("src_hot"), 1)
            V.tensor_tensor(dst_val, iota_c, spread(edst, N), ALU.is_equal).then_inc(ev("dst_hot"), 1)
            dve.wait_ge(ev("upper"), 1)
            dve.wait_ge(ev("keyc"), 1)
            def duplicates(r):
                for c in range(8 * r, 8 * r + 8):
                    if c % TPB == 0:
                        dve.wait_ge(ev("keys_ps"), c // TPB + 1)
                    if c:
                        dve.wait_ge(ev("dup"), c)
                    b = 6 + (c // TPB) % 2
                    V.scalar_tensor_tensor(junk[:, :], bank[b][:, (c % TPB) * P:(c % TPB + 1) * P], keyc[:, c:c + 1],
                                           upper[:, :], ALU.is_equal, ALU.mult, accum_out=dup[:, c:c + 1])\
                        .then_inc(ev("dup"), 1)

            low_weights(0, 4)
            duplicates(0)
            low_weights(4, 8)
            duplicates(1)
            rows_plus_bias("mk", (0, 1), mkb_rows, kf_rows, "kf_rows")
            features_begin(kf_rows[:, :], kf_neg, "kf_rows", "mk")
            duplicates(2)
            features_end(kf_rows[:, :], kf_exp, "mk")
            dve.wait_ge(ev("dup"), EC)
            V.scalar_tensor_tensor(code[:, :], dup[:, :], 0.0, code[:, :], ALU.is_equal, ALU.mult).then_inc(ev("code"), 1)
            dve.wait_ge(ev("code"), 3)
            dve.wait_ge(ev("dst_hot"), 1)
            V.tensor_tensor(dst_val, dst_val, spread(code[:, :], N), ALU.mult).then_inc(ev("dst_val"), 1)
            dve.wait_ge(ev("etw_ln"), 1)
            V.scalar_tensor_tensor(wmask[:, :], etw_sb[:, :], 0.0, sp_a[:, :], ALU.max, ALU.add).then_inc(ev("wmask"), 1)

            low_weights(8, 13)
            dve.wait_ge(ev("edge_ps"), 1)
            V.tensor_copy(esum[:, :], bank[6][0:N, 0:N]).then_inc(ev("esum"), 1)
            dve.wait_ge(ev("ident"), 1)
            V.tensor_scalar(ediag[:, :], ident[0:N, 0:N], 4.0, None, ALU.mult).then_inc(ev("ediag"), 1)
            V.tensor_scalar(far[:, :], ident[0:N, 0:N], FAR, -FAR, ALU.mult, ALU.add).then_inc(ev("far"), 1)
            dve.wait_ge(ev("esum"), 1)
            V.tensor_scalar(ecode[:, :], esum[:, :].bitcast(I32), 22, 7, ALU.logical_shift_right, ALU.bitwise_and)\
                .then_inc(ev("ecode"), 1)
            V.tensor_scalar(absent[:, :], esum[:, :], 0.0, None, ALU.is_equal).then_inc(ev("absent"), 1)
            dve.wait_ge(ev("absent"), 1)
            dve.wait_ge(ev("far"), 1)
            V.tensor_tensor(mtmp[:, :], absent[:, :], ediag[:, :], ALU.mult).then_inc(ev("mtmp"), 1)
            V.tensor_tensor(absent[:, :], absent[:, :], far[:, :], ALU.mult).then_inc(ev("absent"), 1)
            dve.wait_ge(ev("mtmp"), 1)
            dve.wait_ge(ev("ecode"), 1)
            V.tensor_tensor(ecodef[:, :], ecode[:, :], mtmp[:, :], ALU.add).then_inc(ev("ecodef"), 1)
            dve.wait_ge(ev("ecodef"), 1)
            dve.wait_ge(ev("wmask"), 1)
            prev = absent
            for i, c in enumerate((0, 2, 3, 4)):
                if i:
                    dve.wait_ge(ev("mask"), i)
                V.tensor_scalar(mtmp[:, :], ecodef[:, :], float(c), wmask[:, i:i + 1], ALU.is_equal, ALU.mult)\
                    .then_inc(ev("mtmp"), 1)
                dve.wait_ge(ev("mtmp"), 2 + i)
                dve.wait_ge(ev("absent"), 2)
                V.tensor_tensor(mask[:, :], prev[:, :], mtmp[:, :], ALU.add).then_inc(ev("mask"), 1)
                prev = mask

            features_begin(mqT[:, :, :], negT[:, :, :], "mqT", "mq")
            low_weights(13, 16)
            rows_plus_bias("mv", (0, 1), mvb_rows, mv_rows, "mv_rows")

            def max_rhs(c):
                dve.wait_ge(ev(f"rhs_full{c % 2}"), 16 * (c // 2 + 1))
                V.tensor_reduce(ramax[:, c % 2, :], rhs_stage[:, c % 2, :].rearrange("p (k n) -> p n k", k=KT),
                                AX.X, ALU.max, apply_absolute_value=True).then_inc(ev("rhs_pmax"), 1)

            def scale_rhs(c):
                st = rhs_stage[:, c % 2, :].rearrange("p (k n) -> p k n", k=KT)
                dve.wait_ge(ev("rhs_amax"), c + 1)
                sc = rscale[:, c * 256:(c + 1) * 256]
                V.tensor_scalar(sc, ramax[:, c % 2, :], ABSMAX_FLOOR, 1.0 / INT8_MAX, ALU.max, ALU.mult)\
                    .then_inc(ev("rhs_scale"), 1)
                dve.wait_ge(ev("rhs_scale"), c + 1)
                V.reciprocal(rinv[:, c % 2, :], sc).then_inc(ev("rhs_inv"), 1)
                dve.wait_ge(ev("rhs_inv"), c + 1)
                V.tensor_tensor(st, st, rinv[:, c % 2, :].unsqueeze(1).to_broadcast([P, KT, 256]), ALU.mult)\
                    .then_inc(ev("rhs_div"), 1)
                dve.wait_ge(ev("rhs_div"), c + 1)
                V.tensor_scalar(st, st, INT8_MAX, -INT8_MAX, ALU.min, ALU.max).then_inc(ev("rhs_scaled"), 1)

            max_rhs(0)
            features_end(mqT[:, :, :], expT[:, :, :], "mq")
            dve.wait_ge(ev("z_ps"), 1)
            V.tensor_copy(z_sb[:, :], bank[6][:, 0:KT]).then_inc(ev("z_sb"), 1)
            dve.wait_ge(ev("z_sb"), 1)
            dve.wait_ge(ev("blockm"), 2)
            V.tensor_tensor(kvz[:, 1, :, :], blockm[:, :].unsqueeze(1).to_broadcast([P, KT, P]),
                            spread(z_sb[:, :], P), ALU.mult).then_inc(ev("kv"), 1)
            for h in range(2):
                dve.wait_ge(ev("kv_ps"), h + 1)
                V.tensor_tensor(kvz[:, 0, TPB * h:TPB * (h + 1), :], bank[4 + h][:, :].rearrange("p (j n) -> p j n", j=TPB),
                                blockm[:, :].unsqueeze(1).to_broadcast([P, TPB, P]), ALU.mult).then_inc(ev("kv"), 1)
            max_rhs(1)
            scale_rhs(0)
            scale_rhs(1)
            for h in range(2):
                js = slice(TPB * h, TPB * (h + 1))
                dve.wait_ge(ev("den_ps"), h + 1)
                V.tensor_scalar(negT[:, js, :], tiles(6 + h), ATTN_EPS, None, ALU.max).then_inc(ev("den"), 1)
            dve.wait_ge(ev("den"), 2)
            V.reciprocal(negT[:, :, :], negT[:, :, :]).then_inc(ev("rden"), 1)
            dve.wait_ge(ev("rden"), 1)
            for h in range(2):
                js = slice(TPB * h, TPB * (h + 1))
                V.tensor_tensor(yT[:, js, :], tiles(4 + h), negT[:, js, :], ALU.mult).then_inc(ev("yT"), 1)
            for c in (2, 3):
                max_rhs(c)
                scale_rhs(c)

            dve.wait_ge(ev("mask"), 4)

            def shift_scores(g):
                hs = group_heads(g)
                pg = probs[:, hs[0]:hs[-1] + 1:2, :]
                mx = smax[:, 4 * g:4 * g + 4]
                dve.wait_ge(ev("scores_ps"), g + 1)
                V.scalar_tensor_tensor(pg, tiles(4 + g)[0:N, :, :], float(HD) ** -0.5,
                                       mask[:, :].unsqueeze(1).to_broadcast([N, 4, N]), ALU.mult, ALU.add)\
                    .then_inc(ev("scores"), 1)
                dve.wait_ge(ev("scores"), g + 1)
                V.tensor_reduce(mx, pg, AX.X, ALU.max).then_inc(ev("smax"), 1)
                dve.wait_ge(ev("smax"), g + 1)
                V.tensor_tensor(pg, pg, spread(mx, N), ALU.subtract).then_inc(ev("scores_shifted"), 1)

            def normalise(g):
                hs = group_heads(g)
                pg = probs[:, hs[0]:hs[-1] + 1:2, :]
                sm = ssum[:, 4 * g:4 * g + 4]
                rs = rsum[:, 4 * g:4 * g + 4]
                dve.wait_ge(ev("probs_exp"), g + 1)
                V.tensor_reduce(sm, pg, AX.X, ALU.add).then_inc(ev("ssum"), 1)
                dve.wait_ge(ev("ssum"), g + 1)
                V.reciprocal(rs, sm).then_inc(ev("rsum"), 1)
                dve.wait_ge(ev("rsum"), g + 1)
                V.tensor_tensor(pg, pg, spread(rs, N), ALU.mult).then_inc(ev("probs"), 1)

            shift_scores(0)
            for g in range(1, 4):
                shift_scores(g)
                normalise(g - 1)
            normalise(3)
            low_weights(18, 22)
            for g in (0, 2):
                hs = group_heads(g)
                dve.wait_ge(ev("probs_tr"), g + 1)
                V.tensor_copy(probsT[:, hs[0]:hs[-1] + 1:2, :], tiles(4 + g)[0:N, :, :]).then_inc(ev("probsT_even"), 1)
            low_weights(22, 26)
            dve.wait_ge(ev("xn_outb"), 1)
            for h in range(2):
                cs = slice(h * HALF, (h + 1) * HALF)
                dve.wait_ge(ev("chunk_done"), chunk_count("ow", 3))
                V.tensor_tensor(y1_rows[:, cs], bank[2 + h][0:N, :], xn_rows[:, cs], ALU.add).then_inc(ev("y1_rows"), 1)
            low_weights(26, 29)
            dve.wait_ge(ev("base"), 1)
            layer_norm(2, y1_rows[:, :], ln2_rows[:, :], "y1_rows", (1, 2))
            low_weights(29, 32)
            dve.wait_ge(ev("v_low"), 1)
            affine_T((2, 3), ln2T, "g2", "be2", "ln2_tr", "ln2T")
            low_weights(32, 36)
            dve.wait_ge(ev("pv_ps"), 1)
            V.tensor_tensor(aT[:, 0:TPB, :], tiles(4), spread(col("biv", 0, TPB), N), ALU.add).then_inc(ev("aT_a"), 1)
            dve.wait_ge(ev("aT_a"), 1)
            V.tensor_copy(a_parts[:, 0:TPB, 0, 0:N], aT[:, 0:TPB, :]).then_inc(ev("a_high_a"), 1)
            dve.wait_ge(ev("a_high_a"), 1)
            V.tensor_tensor(a_parts[:, 0:TPB, 1, 0:N], aT[:, 0:TPB, :], a_parts[:, 0:TPB, 0, 0:N], ALU.subtract)\
                .then_inc(ev("a_low"), 1)
            dve.wait_ge(ev("a_high"), 1)
            V.tensor_tensor(a_parts[:, TPB:KT, 1, 0:N], aT[:, TPB:KT, :], a_parts[:, TPB:KT, 0, 0:N], ALU.subtract)\
                .then_inc(ev("a_low"), 1)
            low_weights(36, 40)

            dve.wait_ge(ev("base"), 3)
            mean = mv[:, 3, 0:1]
            for i, (b, c0, width) in enumerate(PIECES):
                cs = slice(c0, c0 + width)
                dve.wait_ge(ev("wo_ps"), i + 1)
                V.tensor_tensor(x1_rows[:, cs], bank[b][0:N, 0:width], base_rows[:, cs], ALU.add).then_inc(ev("x1"), 1)
                dve.wait_ge(ev("x1"), i + 1)
                for c in range(c0 // QUARTER, (c0 + width) // QUARTER):
                    V.bn_stats(stats_x1[:, c, :], x1_rows[:, c * QUARTER:(c + 1) * QUARTER]).then_inc(ev("bn_x1"), 1)
                V.tensor_reduce(extremes[:, 0, i:i + 1], x1_rows[:, cs], AX.X, ALU.max).then_inc(ev("x1_max"), 1)
                if i == len(PIECES) - 1:
                    dve.wait_ge(ev("bn_x1"), 4)
                    V.bn_aggr(mv[:, 3, :], stats_x1[:, :, :]).then_inc(ev("ln_stats"), 1)
                V.tensor_reduce(extremes[:, 1, i:i + 1], x1_rows[:, cs], AX.X, ALU.min).then_inc(ev("x1_min"), 1)
            amax, scale, qs, ls = (lscale[:, i:i + 1] for i in range(4))
            dve.wait_ge(ev("x1_min"), 4)
            dve.wait_ge(ev("ln_stats"), 4)
            V.tensor_scalar(extremes[:, 0, :], extremes[:, 0, :], mean, 1.0 / INT8_MAX, ALU.subtract, ALU.mult)\
                .then_inc(ev("spread"), 1)
            V.tensor_scalar(extremes[:, 1, :], extremes[:, 1, :], mean, -1.0 / INT8_MAX, ALU.subtract, ALU.mult)\
                .then_inc(ev("spread"), 1)
            dve.wait_ge(ev("spread"), 2)
            V.tensor_reduce(amax, extremes[:, :, :], AX.XY, ALU.max).then_inc(ev("lq"), 1)
            dve.wait_ge(ev("ln_sd"), 4)
            dve.wait_ge(ev("lq"), 1)
            V.scalar_tensor_tensor(scale, sd[:, 3:4], ABSMAX_FLOOR / INT8_MAX, amax, ALU.mult, ALU.max).then_inc(ev("lq"), 1)
            dve.wait_ge(ev("lq"), 2)
            V.reciprocal(qs, scale).then_inc(ev("lq"), 1)
            dve.wait_ge(ev("lq"), 3)
            for h in range(2):
                cs = slice(h * HALF, (h + 1) * HALF)
                V.tensor_scalar(xl_rows[:, cs], x1_rows[:, cs], mean, qs, ALU.subtract, ALU.mult).then_inc(ev("lq"), 1)
            for h in range(2):
                cs = slice(h * HALF, (h + 1) * HALF)
                dve.wait_ge(ev("lq"), 4 + h)
                V.tensor_scalar(xl_rows[:, cs], xl_rows[:, cs], ROUND, ROUND + INT8_MAX, ALU.add, ALU.min)\
                    .then_inc(ev("lq_magic"), 1)
            for h in range(2):
                cs = slice(h * HALF, (h + 1) * HALF)
                dve.wait_ge(ev("lq_magic"), h + 1)
                V.tensor_scalar(q_rows[:, cs], xl_rows[:, cs], ROUND - INT8_MAX, -ROUND, ALU.max, ALU.add)\
                    .then_inc(ev("q_rows"), 1)
            dve.wait_ge(ev("q8_tr"), 1)
            V.tensor_copy(q8T[:, 0:TPB, :], bank[4][:, 0:TPB * N // 2].bitcast(BF16)
                          .rearrange("p (j n) -> p j n", j=TPB)).then_inc(ev("q8T_a"), 1)
            V.reciprocal(rstd[:, 3:4], sd[:, 3:4]).then_inc(ev("ln_rstd"), 1)
            dve.wait_ge(ev("ln_rstd"), 4)
            V.tensor_tensor(ls, scale, rstd[:, 3:4], ALU.mult).then_inc(ev("ls"), 1)
            dve.wait_ge(ev("ls"), 1)
            V.tensor_scalar(xl_rows[:, :], rscale[0:N, :], ls, None, ALU.mult).then_inc(ev("scales"), 1)
            dve.wait_ge(ev("scales"), 1)
            for c in range(4):
                cs = slice(c * QUARTER, (c + 1) * QUARTER)
                dve.wait_ge(ev("ffn_ps"), c + 1)
                V.tensor_tensor(xl_rows[:, cs], bank[FFN_BANKS[c]][0:N, 0:QUARTER],
                                xl_rows[:, cs], ALU.mult).then_inc(ev("ffn"), 1)
                if c >= 2:
                    dve.wait_ge(ev("ffn"), c + 1)
                    V.tensor_tensor(x1_rows[:, cs], x1_rows[:, cs], xl_rows[:, cs], ALU.add).then_inc(ev("out_ready"), 1)

        @block.tensor
        def _(pe):
            T = nc.tensor

            def chunk_arrived(w, q):
                c = FIRST[w] + q
                pe.wait_ge(ev(f"slot_full{c % RING}"), 16 * (c // RING + 1))

            def project_T(w, src, banks, q):
                chunk_arrived(w, q)
                for j in (2 * q, 2 * q + 1):
                    for k in range(KT):
                        ins = T.matmul(tiles(banks[j // TPB])[:, j % TPB, :],
                                       slot(w, q)[:, ((j % 2) * KT + k) * P:((j % 2) * KT + k + 1) * P],
                                       src[:, k, :], start=(k == 0), stop=(k == KT - 1))
                ins.then_inc(ev("chunk_done"), 1)

            def rows_to_T(src, banks, name):
                for h in range(2):
                    for j in range(TPB * h, TPB * h + TPB):
                        ins = T.transpose(tiles(banks[h])[:, j % TPB, :], src[:, j * P:(j + 1) * P], ident[0:N, 0:N])
                    ins.then_inc(ev(name), 1)

            def split_products(u, parts, out, cols, first, last):
                k = u % KT
                w_high, w_low = (w[:, u % PART_BUFS, cols] for w in (w_hi, w_lo))
                T.matmul(out, parts[:, k, 0, :], w_high, start=first, stop=False, skip_group_check=True)
                T.matmul(out, parts[:, k, 0, :], w_low, start=False, stop=False, skip_group_check=True)
                return T.matmul(out, parts[:, k, 1, :], w_high, start=False, stop=last, skip_group_check=True)

            def unit_ready(u):
                pe.wait_ge(ev("w_low_pool" if u in POOL_UNITS else "w_low_dve"), low_count(u))

            def project_rows(w, parts, banks, q):
                for u in (UNIT0[w] + 2 * q, UNIT0[w] + 2 * q + 1):
                    unit_ready(u)
                    for h in range(2):
                        ins = split_products(u, parts, bank[banks[h]][:, :], slice(h * HALF, (h + 1) * HALF),
                                             u % KT == 0, u % KT == KT - 1)
                    ins.then_inc(ev("chunk_done" if u % 2 else "half_done"), 1)

            def keys(r):
                if r:
                    pe.wait_ge(ev("dup"), 8 * r)
                for b in range(2):
                    o = (2 * r + b) * HALF
                    T.matmul(bank[6 + b][:, :], keyw[:, :], keyrow[:, o:o + HALF], start=True, stop=True)\
                        .then_inc(ev("keys_ps"), 1)

            def warm_up(n):
                for _ in range(n):
                    T.matmul(bank[5][:, 0:P], ones[:, :], ones[:, :], start=True, stop=True)

            pe.wait_ge(ev("ones"), 1)
            warm_up(HEAD_WARM)
            pe.wait_ge(ev("ident"), 1)
            pe.wait_ge(ev("ln_done"), 1)
            rows_to_T(xn_rows, (0, 1), "xn_tr")

            pe.wait_ge(ev("xnT_a"), 1)
            pe.wait_ge(ev("xnT_b"), 1)
            project_T("q", xnT, (2, 3), 0)
            pe.wait_ge(ev("ln_done"), 2)
            rows_to_T(ln_rows, (4, 5), "lnx_tr")
            project_T("q", xnT, (2, 3), 1)
            pe.wait_ge(ev("keyrow"), 1)
            pe.wait_ge(ev("keyw"), 1)
            keys(0)
            project_T("q", xnT, (2, 3), 2)
            project_T("q", xnT, (2, 3), 3)

            pe.wait_ge(ev("padding"), 2)
            pe.wait_ge(ev("ln_low"), 1)
            project_rows("mk", ln_parts, (0, 1), 0)
            project_rows("mk", ln_parts, (0, 1), 1)
            keys(1)
            project_rows("mk", ln_parts, (0, 1), 2)
            project_rows("mk", ln_parts, (0, 1), 3)

            pe.wait_ge(ev("qT"), 2)
            project_T("mq", lnT, (2, 3), 0)
            keys(2)
            project_T("mq", lnT, (2, 3), 1)
            project_T("mq", lnT, (2, 3), 2)
            pe.wait_ge(ev("src_hot"), 1)
            pe.wait_ge(ev("dst_val"), 1)
            for c in range(EC):
                ins = T.matmul(bank[6][0:N, 0:N], src_hot[:, c, :], dst_val[:, c, :], start=(c == 0), stop=(c == EC - 1))
            ins.then_inc(ev("edge_ps"), 1)
            project_T("mq", lnT, (2, 3), 3)

            pe.wait_ge(ev("kf_rows"), 2)
            for q in range(4):
                project_rows("mv", ln_parts, (0, 1), q)

            pe.wait_ge(ev("mqT"), 2)
            project_T("k", xnT, (2, 3), 0)
            project_T("k", xnT, (2, 3), 1)
            pe.wait_ge(ev("mv_rows"), 2)
            pe.wait_ge(ev("mk_feat"), 1)
            pe.wait_ge(ev("esum"), 1)
            for j in range(KT):
                js = slice(j * P, (j + 1) * P)
                ins = T.matmul(bank[4 + j // TPB][:, (j % TPB) * P:(j % TPB + 1) * P], kf_rows[:, js], mv_rows[:, js],
                               start=True, stop=True)
                if j % TPB == TPB - 1:
                    ins.then_inc(ev("kv_ps"), 1)
            for j in range(KT):
                ins = T.matmul(bank[6][:, j:j + 1], kf_rows[:, j * P:(j + 1) * P], ones[0:N, 0:1], start=True, stop=True)
            ins.then_inc(ev("z_ps"), 1)
            project_T("k", xnT, (2, 3), 2)
            project_T("k", xnT, (2, 3), 3)

            project_T("q2", qT, (0, 1), 0)
            pe.wait_ge(ev("kv"), 3)
            pe.wait_ge(ev("mq_feat"), 1)
            for what in range(2):
                for j in range(KT):
                    ins = T.matmul(tiles(4 + 2 * what + j // TPB)[:, j % TPB, :], kvz[:, what, j, :], mqT[:, j, :],
                                   start=True, stop=True)
                    if what == 1 and j % TPB == TPB - 1:
                        ins.then_inc(ev("den_ps"), 1)
            for q in range(1, 4):
                project_T("q2", qT, (0, 1), q)

            pe.wait_ge(ev("kT"), 2)
            for q in range(4):
                project_T("k2", kT, (2, 3), q)

            pe.wait_ge(ev("q2T"), 2)
            project_T("v", xnT, (0, 1), 0)
            pe.wait_ge(ev("yT"), 2)
            pe.wait_ge(ev("k2T"), 2)
            for g in range(4):
                for i, h in enumerate(group_heads(g)):
                    r = slice(HD * (h % 2), HD * (h % 2) + HD)
                    ins = T.matmul(tiles(4 + g)[0:N, i, :], q2T[r, h // 2, :], k2T[r, h // 2, :], start=True, stop=True)
                ins.then_inc(ev("scores_ps"), 1)
            for q in range(1, 4):
                project_T("v", xnT, (0, 1), q)

            def turn_probs(g):
                pe.wait_ge(ev("probs"), g + 1)
                for i, h in enumerate(group_heads(g)):
                    ins = T.transpose(tiles(4 + g)[0:N, i, :], probs[:, h, :], ident[0:N, 0:N])
                ins.then_inc(ev("probs_tr"), 1)

            pe.wait_ge(ev("padding"), 2)
            pe.wait_ge(ev("y_low"), 1)
            project_rows("ow", y_parts, (2, 3), 0)
            project_rows("ow", y_parts, (2, 3), 1)
            for g in range(4):
                turn_probs(g)
            project_rows("ow", y_parts, (2, 3), 2)
            project_rows("ow", y_parts, (2, 3), 3)

            pe.wait_ge(ev("vT"), 2)
            pe.wait_ge(ev("v_low"), 1)
            for q in range(3):
                project_rows("v2", v_parts, (0, 1), q)
            pe.wait_ge(ev("ln_done"), 3)
            rows_to_T(ln2_rows, (2, 3), "ln2_tr")
            project_rows("v2", v_parts, (0, 1), 3)

            pe.wait_ge(ev("ln2T"), 2)
            pe.wait_ge(ev("probsT_even"), 2)
            chunk_arrived("w12", 0)
            w1 = slot("w12", 0)[:, 0:D]
            w2 = slot("w12", 0)[:, D:2 * D]
            for k in range(KT):
                ins = T.matmul(bank[6][:, 0:N], w1[:, k * P:(k + 1) * P], ln2T[:, k, :], start=(k == 0), stop=(k == KT - 1))
            ins.then_inc(ev("h_ps"), 1)
            pe.wait_ge(ev("v2_rows"), 2)
            pe.wait_ge(ev("probsT_odd"), 2)
            for h in range(H):
                r = slice(HD * (h % 2), HD * (h % 2) + HD)
                ins = T.matmul(tiles(4 + h // 8)[r, (h % 8) // 2, :], v2_rows[:, h * HD:(h + 1) * HD], probsT[:, h, :],
                               start=True, stop=True)
                if h % 8 == 7:
                    ins.then_inc(ev("pv_ps"), 1)
            pe.wait_ge(ev("hT"), 1)
            for b, c0, width in PIECES:
                ins = T.matmul(bank[b][0:N, 0:width], hT[:, :], w2[:, c0:c0 + width], start=True, stop=False,
                               skip_group_check=True)
            ins.then_inc(ev("chunk_done"), 1)

            def wo_products(i, u):
                b, c0, width = PIECES[i]
                return split_products(u, a_parts, bank[b][:, 0:width], slice(c0, c0 + width), False, u == UNITS - 1)

            for u in range(UNIT0["wo"], UNITS - PIECE_UNITS):
                unit_ready(u)
                pe.wait_ge(ev("a_low"), 1 + (u % KT) // TPB)
                for i in range(len(PIECES)):
                    ins = wo_products(i, u)
                ins.then_inc(ev("chunk_done" if u % 2 else "half_done"), 1)
            pe.wait_ge(ev("a_low"), 2)
            for i in range(len(PIECES)):
                for u in range(UNITS - PIECE_UNITS, UNITS):
                    if i == 0:
                        unit_ready(u)
                    ins = wo_products(i, u)
                ins.then_inc(ev("wo_ps"), 1)
            pe.wait_ge(ev("rhs_rounded"), 4)
            for _ in range(TAIL_WARM):
                T.matmul(bank[5][:, :], rhs_q[:, 0, 0:P], rhs_q[:, 0, 0:HALF], start=True, stop=True)

            pe.wait_ge(ev("identb"), 1)
            for h in range(2):
                pe.wait_ge(ev("q_rows"), h + 1)
                for j in range(TPB * h, TPB * h + TPB):
                    ins = T.transpose(bank[4 + h][:, 0:TPB * N // 2].bitcast(BF16)[:, (j % TPB) * N:(j % TPB + 1) * N],
                                      q_rows[:, j * P:(j + 1) * P], identb[0:N, 0:N])
                ins.then_inc(ev("q8_tr"), 1)
            for c, k0 in ((0, 0), (1, 0), (0, TPB), (1, TPB), (2, 0), (2, TPB), (3, 0), (3, TPB)):
                pe.wait_ge(ev("q8T_b" if k0 else "q8T_a"), 1)
                for k in range(k0, k0 + TPB):
                    ins = T.matmul(bank[FFN_BANKS[c]][0:N, 0:QUARTER], q8T[:, k, :],
                                   rhs_q[:, c, k * QUARTER:(k + 1) * QUARTER], start=(k == 0), stop=(k == KT - 1),
                                   skip_group_check=True)
                if k0:
                    ins.then_inc(ev("ffn_ps"), 1)


def kernel(**inputs):
    import numpy as np
    from concourse import bacc
    from concourse.bass_utils import run_bass_kernel_spmd

    a = {k: np.ascontiguousarray(v) for k, v in inputs.items()}
    g, m = "L0_gnn_", "L0_mix_"

    def blocks_T(w):
        return w.reshape(KT, P, 4, 2, P).transpose(2, 1, 3, 0, 4).reshape(4, P, CHUNK)

    def blocks_rows(w):
        return w.reshape(4, 2, P, D).transpose(0, 2, 1, 3).reshape(4, P, CHUNK)

    qkv = a[m + "qkv_w"]
    parts = {
        "q": blocks_T(a[g + "wq"].T), "k": blocks_T(a[g + "wk"].T), "v": blocks_T(a[g + "wv"].T),
        "q2": blocks_T(a[g + "wiq"].T), "k2": blocks_T(a[g + "wik"].T), "v2": blocks_rows(a[g + "wiv"].T),
        "mq": blocks_T(qkv[:, 0:D]), "mk": blocks_rows(qkv[:, D:2 * D]), "mv": blocks_rows(qkv[:, 2 * D:3 * D]),
        "ow": blocks_rows(a[m + "out_w"]), "wo": blocks_rows(a[g + "wo"].T),
        "w12": np.concatenate([a[m + "w1"].reshape(KT, P, P).transpose(1, 0, 2).reshape(P, D), a[m + "w2"]], axis=1)[None],
    }
    weights = np.ascontiguousarray(np.concatenate([parts[w] for w in ORDER]))
    vectors = {
        "bq": a[g + "bq"], "bk": a[g + "bk"], "bv": a[g + "bv"], "biq": a[g + "biq"], "bik": a[g + "bik"],
        "biv": a[g + "biv"], "mqb": a[m + "qkv_b"][0:D],
        "g1": a[m + "g1"], "be1": a[m + "be1"], "g2": a[m + "g2"], "be2": a[m + "be2"],
    }
    arrays = {
        "x_in": a["x"],
        "weights": weights,
        "rhs": np.ascontiguousarray(a["L0_ffn_rhs"].reshape(KT, P, 4, 256).transpose(2, 1, 0, 3).reshape(4, P, CHUNK)),
        "cols": np.ascontiguousarray(np.concatenate([vectors[n].reshape(KT, P).T for n in COLS] + [a[m + "b1"][:, None]], axis=1)),
        "row_vectors": np.ascontiguousarray(np.broadcast_to(
            np.stack([a[m + "qkv_b"][D:2 * D], a[m + "qkv_b"][2 * D:], a[g + "bo"], a[m + "b2"], a[m + "out_b"]])[:, None, :],
            (5, N, D))),
        "edge_cols": np.ascontiguousarray(np.stack([a[n].reshape(EC, P).T for n in ("src", "dst", "edge_type_5")], axis=1)),
        "edge_rows": np.ascontiguousarray(np.stack([a["src"], a["dst"]])),
        "etw": np.ascontiguousarray(np.broadcast_to(a[g + "edge_type_weights"], (N, 4))),
    }
    nc = bacc.Bacc("TRN2", target_bir_lowering=False, num_devices=1)
    aps = [nc.dram_tensor(n, v.shape, mybir.dt.from_np(v.dtype), kind="ExternalInput").ap() for n, v in arrays.items()]
    out = nc.dram_tensor("out_rows", (N, D), F32, kind="ExternalOutput").ap()
    build(nc, *aps, out)
    r = run_bass_kernel_spmd(nc, [arrays], core_ids=[0])
    return r.results[0]["out_rows"]
```
